# Optimizing a Trainium2 kernel written in Bass

```python
import numpy as np
import jax
import jax.numpy as jnp

def _softmax(x, axis=-1):
    return jax.nn.softmax(x, axis=axis)

def _gelu(x):
    return jax.nn.gelu(x, approximate=True)

def _silu(x):
    return jax.nn.silu(x)

def _sigmoid(x):
    return jax.nn.sigmoid(x)

def _layernorm(x, axis=-1, eps=1e-05):
    m = jnp.mean(x, axis=axis, keepdims=True)
    v = jnp.var(x, axis=axis, keepdims=True)
    return (x - m) / jnp.sqrt(v + eps)

def _scatter_add(tgt, idx, src, axis=0):
    return tgt.at[idx].add(src)

def _segment_sum(src, seg, n):
    return jax.ops.segment_sum(src, seg, n)
kernel_name = 'mk_adaln_ffn_d1_seqx_r4_276686'

def setup_inputs(seed: int=0):
    np.random.seed(seed)
    _w = jnp.asarray

    def _rec_inputs():
        import jax
        import jax.numpy as jnp
        _rk = jax.random.key(seed)
        x = -7.109e-05 + 0.9999 * jax.random.normal(jax.random.fold_in(_rk, 1), (32, 64, 1024), jnp.float32)
        _lenS = 64 - jax.random.randint(jax.random.fold_in(_rk, 7), (32,), 0, max(1, 64 // 4) + 1, jnp.int32)
        _lenS2 = 64 - jax.random.randint(jax.random.fold_in(_rk, 8), (32,), 0, max(1, 64 // 4) + 1, jnp.int32)
        itok_B_0_15 = jax.random.randint(jax.random.fold_in(_rk, 11), (32,), 0, 16, jnp.int32)
        return (x, itok_B_0_15)
    x, itok_B_0_15 = _rec_inputs()

    def _L0_cond_setup():
        import jax, jax.numpy as jnp
        import numpy as np
        NUM_CONDITIONS = 16
        IN_CH = 64
        OUT_CH = 64
        B = 64
        T = 1024
        key = jax.random.key(seed)
        k_x, k_w, k_c = jax.random.split(key, 3)
        x = jax.random.normal(k_x, (B, IN_CH, T), dtype=jnp.float32)
        bound = float(np.sqrt(6.0 / IN_CH))
        weights = jax.random.uniform(k_w, (NUM_CONDITIONS, IN_CH, OUT_CH), dtype=jnp.float32, minval=-bound, maxval=bound)
        condition = jax.random.randint(k_c, (B,), 0, NUM_CONDITIONS, dtype=jnp.int64)
        return {'x': x, 'weights': weights, 'condition': condition}
    _L0_cond_all = _L0_cond_setup()
    _L0_cond_in = {k: v for k, v in _L0_cond_all.items() if k in ('weights',)}
    del _L0_cond_all

    def _L0_ffn_setup():
        import jax, jax.numpy as jnp
        import numpy as np
        _TRIPLES = [(1, 2, 3), (1, 4, 5), (1, 7, 6), (2, 4, 6), (2, 5, 7), (3, 4, 7), (3, 6, 5)]

        def _oct_struct():
            S = np.zeros((8, 8, 8), np.float32)
            S[0, 0, 0] = 1.0
            for i in range(1, 8):
                S[0, i, i] = 1.0
                S[i, 0, i] = 1.0
                S[i, i, 0] = -1.0
            for a, b, c in _TRIPLES:
                for x, y, z in ((a, b, c), (b, c, a), (c, a, b)):
                    S[x, y, z] = 1.0
                    S[y, x, z] = -1.0
            return jnp.asarray(S)
        S_OCT = _oct_struct()
        N_EMBD = 1024
        HIDDEN = 2732

        def ternary_dequant(W):
            scale = jnp.mean(jnp.abs(W))
            Wq = scale * jnp.clip(jnp.round(W / scale), -1.0, 1.0)
            return W + jax.lax.stop_gradient(Wq - W)

        def oct_ternary_linear(xp, W):
            Wq = ternary_dequant(W)
            M = jnp.einsum('jik,jod->koid', S_OCT, Wq)
            return jnp.einsum('...id,koid->...ko', xp, M)
        key = jax.random.key(seed)
        k1, k2, k3, k4 = jax.random.split(key, 4)
        B, T = (2, 512)
        d8, h8 = (N_EMBD // 8, HIDDEN // 8)
        std_in = 1.0 / np.sqrt(N_EMBD)
        std_h = 1.0 / np.sqrt(HIDDEN)
        return {'x': jax.random.normal(k1, (B, T, N_EMBD), jnp.float32), 'w_gate': jax.random.normal(k2, (8, h8, d8), jnp.float32) * std_in, 'w_up': jax.random.normal(k3, (8, h8, d8), jnp.float32) * std_in, 'w_down': jax.random.normal(k4, (8, d8, h8), jnp.float32) * std_h}
    _L0_ffn_all = _L0_ffn_setup()
    _L0_ffn_in = {k: v for k, v in _L0_ffn_all.items() if k in ('w_gate', 'w_up', 'w_down')}
    del _L0_ffn_all
    return {'x': x, 'itok_B_0_15': itok_B_0_15, 'L0_cond_weights': _L0_cond_in['weights'], 'L0_ffn_w_gate': _L0_ffn_in['w_gate'], 'L0_ffn_w_up': _L0_ffn_in['w_up'], 'L0_ffn_w_down': _L0_ffn_in['w_down']}

def reference(x, itok_B_0_15, L0_cond_weights, L0_ffn_w_gate, L0_ffn_w_up, L0_ffn_w_down):
    import jax
    import jax.numpy as jnp

    def _L0_cond_ref(x, weights, condition):
        import jax, jax.numpy as jnp
        import numpy as np
        NUM_CONDITIONS = 16
        IN_CH = 64
        OUT_CH = 64
        B = 64
        T = 1024
        W = weights[condition]
        return jnp.einsum('bct,bcd->bdt', x, W)

    def _L0_ffn_ref(x, w_gate, w_up, w_down):
        import jax, jax.numpy as jnp
        import numpy as np
        _TRIPLES = [(1, 2, 3), (1, 4, 5), (1, 7, 6), (2, 4, 6), (2, 5, 7), (3, 4, 7), (3, 6, 5)]

        def _oct_struct():
            S = np.zeros((8, 8, 8), np.float32)
            S[0, 0, 0] = 1.0
            for i in range(1, 8):
                S[0, i, i] = 1.0
                S[i, 0, i] = 1.0
                S[i, i, 0] = -1.0
            for a, b, c in _TRIPLES:
                for x, y, z in ((a, b, c), (b, c, a), (c, a, b)):
                    S[x, y, z] = 1.0
                    S[y, x, z] = -1.0
            return jnp.asarray(S)
        S_OCT = _oct_struct()
        N_EMBD = 1024
        HIDDEN = 2732

        def ternary_dequant(W):
            scale = jnp.mean(jnp.abs(W))
            Wq = scale * jnp.clip(jnp.round(W / scale), -1.0, 1.0)
            return W + jax.lax.stop_gradient(Wq - W)

        def oct_ternary_linear(xp, W):
            Wq = ternary_dequant(W)
            M = jnp.einsum('jik,jod->koid', S_OCT, Wq)
            return jnp.einsum('...id,koid->...ko', xp, M)
        B, T, D = x.shape
        xp = x.reshape(B, T, 8, D // 8)
        gate = oct_ternary_linear(xp, w_gate).reshape(B, T, -1)
        up = oct_ternary_linear(xp, w_up).reshape(B, T, -1)
        h = jax.nn.silu(gate) * up
        hp = h.reshape(B, T, 8, h.shape[-1] // 8)
        out = oct_ternary_linear(hp, w_down).reshape(B, T, D)
        return out
    x = x + _L0_ffn_ref(_L0_cond_ref(x, L0_cond_weights, itok_B_0_15), L0_ffn_w_gate, L0_ffn_w_up, L0_ffn_w_down)
    return x

_drawn_inputs = setup_inputs


def setup_inputs(seed=0):
    import zlib

    import numpy as np

    out = dict(_drawn_inputs(seed))
    spreads = {}
    factors = {}
    for name, (base, spread) in spreads.items():
        noise = np.random.default_rng([zlib.crc32(name.encode()), seed]).standard_normal(out[name].shape)
        drawn = base * np.exp(spread * noise) if base else spread * noise
        out[name] = jnp.asarray(drawn.astype(out[name].dtype))
    for name, factor in factors.items():
        out[name] = (out[name] * factor).astype(out[name].dtype)
    return out
```

```python
from contextlib import ExitStack

import concourse.bass as bass
from concourse import mybir

ALU = mybir.AluOpType
ACT = mybir.ActivationFunctionType
F32 = mybir.dt.float32
F16 = mybir.dt.float16
I32 = mybir.dt.int32
AX = mybir.AxisListType

P = 128
TOK = 256
SUB = TOK // P
NP4 = 4

TRIPLES = [(1, 2, 3), (1, 4, 5), (1, 7, 6), (2, 4, 6), (2, 5, 7), (3, 4, 7), (3, 6, 5)]


def octonion_signs():
    s = {(0, 0): 1}
    for i in range(1, 8):
        s[0, i] = 1
        s[i, 0] = 1
        s[i, i] = -1
    for a, b, c in TRIPLES:
        for x, y in ((a, b), (b, c), (c, a)):
            s[x, y] = 1
            s[y, x] = -1
    return [[s[i ^ k, i] for i in range(8)] for k in range(8)]


def block_plan():
    e = octonion_signs()
    plan = {}
    for K in range(NP4):
        for p in range(NP4):
            a, b, c, d = e[K][p], e[K][p + 4], e[K + 4][p], e[K + 4][p + 4]
            A = K ^ p
            B = A + 4
            if a == d:
                plan[K, p] = {"P": (a, A), "R": [((-a, b, A), p + 4), ((-a, c, A), p)]}
            else:
                assert b == c
                plan[K, p] = {"P": (b, B), "R": [((a, -b, A), p), ((d, -b, A), p + 4)]}
    return plan


def build(nc, x, cond, cond_w, w_gate, w_up, w_down, out):
    NB, C, D = x.shape
    H8, D8 = w_gate.shape[1], w_gate.shape[2]
    NT = NB * C // TOK
    BPT = TOK // C
    assert D8 == P and D == 8 * P and 2 * C == P and w_down.shape == (8, P, H8)
    WIN = [0, P, H8 - P]
    DUP = 2 * P - WIN[2]
    NQ = len(WIN)
    NC = NP4 * NQ
    NOP = 12
    HALF = D // 2
    TOP = float(2 ** 13)

    plan = block_plan()
    slots = {("P", 1, j): j for j in range(8)}
    for (K, p), b in plan.items():
        for key in [("P", *b["P"])] + [("R", *r) for r, _ in b["R"]]:
            slots.setdefault(key, len(slots))
    NSLOT = len(slots)

    xr = x.rearrange("b c t -> (b c) t")
    outr = out.rearrange("b c t -> (b c) t")

    with ExitStack() as ctx:
        def sb(name, shape, dt):
            return ctx.enter_context(nc.sbuf_tensor(name, shape, dt))

        def sem(name):
            return ctx.enter_context(nc.semaphore(name))

        table = [sb("gate_table", [P, NSLOT, NQ, P], F16), sb("up_table", [P, NSLOT, NQ, P], F16)]
        down_w = sb("down_w", [P, NC, 3, NP4, P], F16)
        y_op = sb("y_op", [P, NOP, 2, TOK], F16)
        y_f = sb("y_f", [P, NOP, TOK], F32)
        h_op = sb("h_op", [P, NC, 3, 2, TOK], F16)
        h_f = sb("h_f", [P, NC, 2, TOK], F32)
        h_sum = sb("h_sum", [P, 2, TOK], F32)
        x_in = sb("x_in", [P, SUB, D], F32)
        o_sb = sb("o_sb", [P, SUB, D], F32)
        cond_bd = sb("cond_bd", [P, SUB, P], F32)
        p_sb = sb("p_sb", [P, 2, 2, TOK], F32)
        g_sb = sb("g_sb", [P, 2, 2, TOK], F32)
        s_sb = sb("s_sb", [P, 2, 2, TOK], F32)
        u_sb = sb("u_sb", [P, 2, TOK], F32)
        pd_sb = sb("pd_sb", [P, HALF], F32)
        ident = sb("ident", [P, P], F16)
        ones = sb("ones", [P, P], F32)
        ones_w2 = sb("ones_w2", [P, P], F32)
        idx_sb = sb("idx_sb", [1, NB], I32)
        small = sb("small", [P, 64], F32)
        ps = ctx.enter_context(nc.psum_tensor("ps", [P, 8, 512], F32))

        h_op_f32 = h_op[:].rearrange("p a b c t -> p (a b c t)").bitcast(F32)
        h_f_flat = h_f[:].rearrange("p a b t -> p (a b t)")
        raw_n = NQ * 8 * P
        raw = [h_op_f32[:, 0:raw_n].rearrange("p (w j d) -> p w j d", w=NQ, j=8),
               h_op_f32[:, raw_n:2 * raw_n].rearrange("p (w j d) -> p w j d", w=NQ, j=8)]
        raw_down = h_op_f32[:, 2 * raw_n:2 * raw_n + 8 * H8].rearrange("p (j d) -> p j d", j=8)
        junk = h_f_flat[:, 0:raw_n]
        tern = [h_f_flat[:, raw_n:raw_n + raw_n // 2].bitcast(F16).rearrange("p (w j d) -> p w j d", w=NQ, j=8),
                h_f_flat[:, raw_n + raw_n // 2:2 * raw_n].bitcast(F16).rearrange("p (w j d) -> p w j d", w=NQ, j=8)]
        tern_down = o_sb[:].rearrange("p a t -> p (a t)")[:, 0:4 * H8].bitcast(F16).rearrange("p (j d) -> p j d", j=8)
        down_t = h_op_f32[:, 0:raw_n // 2].bitcast(F16).rearrange("p (w j d) -> p w j d", w=NQ, j=8)

        def col(n, w=1):
            return small[:, n:n + w]

        abs_sum = [col(0, 2), col(2, 2), col(4)]
        scale = [col(6), col(7), col(8)]
        half = [col(9), col(10), col(11)]
        minus_half = [col(12), col(13), col(14)]
        y_max, y_all, y_pow, y_down, y_up = col(16), col(17), col(18), col(19), col(20)
        gate_scale, up_scale = col(21), col(22)
        h_max1, h_all, h_pow, h_down, h_up, down_scale = col(23), col(24), col(25), col(26), col(27), col(28)
        h_max = col(32, NC)

        def bank_r(s, m):
            return ps[:, 3 * s + m, :].rearrange("p (h t) -> p h t", h=2)

        def bank_p(s):
            return ps[:, 3 * s + 2, :].rearrange("p (m t) -> p m t", m=2)

        def bank_y(r):
            return ps[:, 6 + r % 2, :].rearrange("p (i t) -> p i t", i=2)

        def bank_t(n):
            return ps[:, n, :].bitcast(F16).rearrange("p (j d) -> p j d", j=8)

        w_loaded = [sem("gate_loaded"), sem("up_loaded"), sem("down_loaded")]
        idx_loaded = sem("idx_loaded")
        cond_loaded = sem("cond_loaded")
        x_loaded = sem("x_loaded")
        residual_loaded = sem("residual_loaded")
        out_stored = sem("out_stored")
        consts_set = sem("consts_set")
        ident_set = sem("ident_set")
        cond_zeroed = sem("cond_zeroed")
        abs_summed = sem("abs_summed")
        total_ready = sem("total_ready")
        scale_ready = sem("scale_ready")
        compared = sem("compared")
        tern_ready = sem("tern_ready")
        transposed = sem("transposed")
        turned = sem("turned")
        dup_zeroed = sem("dup_zeroed")
        table_ready = sem("table_ready")
        slots_built = sem("slots_built")
        down_w_ready = sem("down_w_ready")
        y_done = sem("y_done")
        y_copied = sem("y_copied")
        y_summed = sem("y_summed")
        y_max_ready = sem("y_max_ready")
        y_all_ready = sem("y_all_ready")
        y_chain = sem("y_chain")
        y_hi_ready = sem("y_hi_ready")
        y_ready = sem("y_ready")
        products = sem("products")
        p_copied = sem("p_copied")
        g_ready = sem("g_ready")
        u_ready = sem("u_ready")
        silu_ready = sem("silu_ready")
        h_ready = sem("h_ready")
        h_max_ready = sem("h_max_ready")
        h_max1_ready = sem("h_max1_ready")
        h_all_ready = sem("h_all_ready")
        reduce_due = sem("reduce_due")
        h_chain = sem("h_chain")
        down_scale_ready = sem("down_scale_ready")
        h_summed = sem("h_summed")
        h_hi_ready = sem("h_hi_ready")
        h_lo_ready = sem("h_lo_ready")
        down_done = sem("down_done")
        pd_ready = sem("pd_ready")
        r_added = sem("r_added")
        o_ready = sem("o_ready")

        DOWN_BANKS = [0, 1, 2]
        TOTAL_BANK = [0, 3, 3]

        block = ctx.enter_context(nc.Block())

        @block.sync
        def _(sp):
            def load_x(T):
                if not isinstance(T, int) or T > 0:
                    sp.wait_ge(y_done, 4 * T)
                sp.dma_start(x_in[:], xr[bass.ds(T * TOK, TOK), :].rearrange("(s p) t -> p s t", p=P)
                             ).then_inc(x_loaded, 16)

            def load_cond(T):
                for b in range(BPT):
                    h = b % 2
                    which = sp.value_load(idx_sb[0:1, bass.ds(T * BPT + b, 1)], min_val=0,
                                          max_val=cond_w.shape[0] - 1)
                    sp.dma_start(cond_bd[C * h:C * h + C, b // 2, C * h:C * h + C],
                                 cond_w[bass.ds(which, 1), :, :].rearrange("a c d -> (a c) d")
                                 ).then_inc(cond_loaded, 16)

            def load_residual(T, first=False):
                if not first:
                    sp.wait_ge(out_stored, 16 * SUB * T)
                sp.dma_start(o_sb[:], xr[bass.ds(T * TOK, TOK), :].rearrange("(s p) t -> p s t", p=P)
                             ).then_inc(residual_loaded, 16)

            def store(T):
                for s in range(SUB):
                    sp.wait_ge(o_ready, SUB * T + s + 1)
                    sp.dma_start(outr[bass.ds(T * TOK + s * P, P), :], o_sb[:, s, :]).then_inc(out_stored, 16)

            sp.dma_start(idx_sb[:], cond.rearrange("(a b) -> a b", a=1)).then_inc(idx_loaded, 16)
            for w in range(NQ):
                sp.dma_start(raw[0][:, w], w_gate[:, WIN[w]:WIN[w] + P, :].rearrange("j o d -> o j d")
                             ).then_inc(w_loaded[0], 16)
            load_x(0)
            sp.wait_ge(idx_loaded, 16)
            sp.wait_ge(cond_zeroed, 1)
            load_cond(0)
            for w in range(NQ):
                sp.dma_start(raw[1][:, w], w_up[:, WIN[w]:WIN[w] + P, :].rearrange("j o d -> o j d")
                             ).then_inc(w_loaded[1], 16)
            sp.dma_start(raw_down, w_down.rearrange("j o d -> o j d")).then_inc(w_loaded[2], 16)
            load_x(1)
            load_cond(1)
            sp.wait_ge(transposed, 3 * NQ)
            load_residual(0, first=True)
            with sp.Fori(1, NT - 1) as T:
                load_x(T + 1)
                load_cond(T + 1)
                store(T - 1)
                load_residual(T)
            store(NT - 2)
            load_residual(NT - 1)
            store(NT - 1)
            sp.wait_ge(out_stored, 16 * SUB * NT)

        @block.gpsimd
        def _(pool):
            pool.memset(cond_bd[:], 0.0).then_inc(cond_zeroed, 1)
            pool.memset(ones[:], 1.0).then_inc(consts_set, 1)
            pool.memset(ones_w2[:], 1.0).then_inc(consts_set, 1)
            pool.memset(ident[:], 0.0).then_inc(consts_set, 1)
            pool.wait_ge(consts_set, 3)
            pool.memset(ones_w2[0:DUP, :], 0.0).then_inc(consts_set, 1)
            pool.affine_select(out=ident[:], in_=ident[:], compare_op=ALU.not_equal, fill=1.0, base=0,
                               pattern=[[-1, P]], channel_multiplier=1).then_inc(ident_set, 1)

            def all_max_h(T):
                pool.wait_ge(h_max1_ready, T + 1)
                pool.sem_inc(reduce_due, 1)
                pool.partition_all_reduce(h_all, h_max1, P, bass.bass_isa.ReduceOp.max).then_inc(h_all_ready, 1)

            def all_max_y(T):
                pool.wait_ge(y_max_ready, T + 1)
                pool.sem_inc(reduce_due, 1)
                pool.partition_all_reduce(y_all, y_max, P, bass.bass_isa.ReduceOp.max).then_inc(y_all_ready, 1)

            def sum_h(T):
                for c in range(NC):
                    pool.wait_ge(h_ready, NC * T + c + 1)
                    if c >= 2 or not isinstance(T, int) or T > 0:
                        pool.wait_ge(h_lo_ready, 2 * (NC * T + c - 1))
                    pool.tensor_tensor(h_sum[:, c % 2, :], h_f[:, c, 0, :], h_f[:, c, 1, :], ALU.add
                                       ).then_inc(h_summed, 1)

            all_max_y(0)
            all_max_h(0)
            all_max_y(1)
            sum_h(0)
            with pool.Fori(1, NT - 1) as T:
                all_max_h(T)
                all_max_y(T + 1)
                sum_h(T)
            all_max_h(NT - 1)
            sum_h(NT - 1)

        @block.scalar
        def _(act):
            def copy_y(T):
                for r in range(4):
                    act.wait_ge(y_done, 4 * T + r + 1)
                    if not isinstance(T, int) or T > 0:
                        act.wait_ge(y_ready, T)
                    act.activation(y_f[:, 2 * r:2 * r + 2, :], bank_y(r), ACT.Copy).then_inc(y_copied, 1)

            def y_hi(T):
                act.wait_ge(y_chain, 6 * T + 4)
                act.wait_ge(y_summed, T + 1)
                if not isinstance(T, int) or T > 0:
                    act.wait_ge(products, 3 * NC * T)
                act.activation(y_op[:, :, 0, :], y_f[:], ACT.Copy, scale=y_up).then_inc(y_hi_ready, 1)

            def h_hi(T, c):
                if c == 0:
                    act.wait_ge(h_chain, 4 * (T + 1))
                    if not isinstance(T, int) or T > 0:
                        act.wait_ge(down_done, SUB * T)
                act.activation(h_op[:, c, 0:2, 0, :], h_f[:, c], ACT.Copy, scale=h_up).then_inc(h_hi_ready, 1)
                act.wait_ge(h_summed, NC * T + c + 1)
                act.activation(h_op[:, c, 2, 0, :], h_sum[:, c % 2, :], ACT.Copy, scale=h_up
                               ).then_inc(h_hi_ready, 1)

            def chunk(T, c):
                later = not isinstance(T, int) or T > 0
                n = NC * T + c
                act.wait_ge(products, 3 * n + 1)
                if later or c >= 2:
                    act.wait_ge(u_ready, n - 1)
                act.activation(p_sb[:, c % 2], bank_p(c % 2), ACT.Copy).then_inc(p_copied, 1)
                if later:
                    h_hi(T - 1, c)
                act.wait_ge(g_ready, n + 1)
                if later or c >= 2:
                    act.wait_ge(h_ready, n - 1)
                act.activation(s_sb[:, c % 2], g_sb[:, c % 2], ACT.Silu, scale=gate_scale
                               ).then_inc(silu_ready, 1)

            def copy_down(T):
                for s in range(SUB):
                    act.wait_ge(down_done, SUB * T + s + 1)
                    act.wait_ge(down_scale_ready, T + 1)
                    if s > 0 or not isinstance(T, int) or T > 0:
                        act.wait_ge(o_ready, SUB * T + s)
                    act.activation(pd_sb[:].rearrange("p (k o) -> p k o", k=NP4),
                                   ps[:, 3 * s + 2, :].rearrange("p (k o) -> p k o", k=NP4),
                                   ACT.Copy, scale=down_scale).then_inc(pd_ready, 1)

            act.sem_inc(pd_ready, SUB)
            for m in range(2):
                act.wait_ge(w_loaded[m], 16 * NQ)
                if m > 0:
                    act.wait_ge(abs_summed, 2 * m)
                act.activation(junk[:, 0:2 * 8 * P], raw[m][:, 0:2].rearrange("p w j d -> p (w j d)"), ACT.Abs,
                               accum_out=abs_sum[m][:, 0:1]).then_inc(abs_summed, 1)
                act.wait_ge(abs_summed, 2 * m + 1)
                act.activation(junk[:, 2 * 8 * P:raw_n], raw[m][:, 2].rearrange("p j d -> p (j d)"), ACT.Abs,
                               accum_out=abs_sum[m][:, 1:2]).then_inc(abs_summed, 1)
                if m == 0:
                    copy_y(0)
            act.wait_ge(w_loaded[2], 16)
            act.wait_ge(abs_summed, 4)
            act.activation(junk[:, 0:8 * H8], raw_down.rearrange("p j d -> p (j d)"), ACT.Abs,
                           accum_out=abs_sum[2]).then_inc(abs_summed, 1)
            y_hi(0)
            for c in range(NC):
                chunk(0, c)
            copy_y(1)
            y_hi(1)
            with act.Fori(1, NT - 1) as T:
                for c in range(NC):
                    chunk(T, c)
                copy_y(T + 1)
                y_hi(T + 1)
                copy_down(T - 1)
            for c in range(NC):
                chunk(NT - 1, c)
            copy_down(NT - 2)
            for c in range(NC):
                h_hi(NT - 1, c)
            copy_down(NT - 1)

        @block.vector
        def _(dve):
            counts = (8 * H8 * P, 8 * H8 * P, 8 * H8 * P)

            def scales(m):
                dve.wait_ge(total_ready, m + 1)
                for dst, f in ((scale[m], 1.0), (half[m], 0.5), (minus_half[m], -0.5)):
                    dve.tensor_scalar(dst, total(m), f / counts[m], None, ALU.mult).then_inc(scale_ready, 1)

            def total(m):
                return ps[:, TOTAL_BANK[m], 0:1]

            def ternary(m, dst, src):
                dve.wait_ge(scale_ready, 3 * (m + 1))
                dve.tensor_scalar(dst, src, minus_half[m], None, ALU.is_lt).then_inc(compared, 1)
                dve.wait_ge(compared, m + 1)
                dve.scalar_tensor_tensor(out=dst, in0=src, scalar=half[m], in1=dst, op0=ALU.is_gt,
                                         op1=ALU.subtract).then_inc(tern_ready, 1)

            def combine(dst, ta, tb, sa, sb_):
                if sa > 0:
                    return dve.tensor_tensor(dst, ta, tb, ALU.add if sb_ > 0 else ALU.subtract)
                if sb_ > 0:
                    return dve.tensor_tensor(dst, tb, ta, ALU.subtract)
                return dve.scalar_tensor_tensor(out=dst, in0=ta, scalar=-1.0, in1=tb, op0=ALU.mult,
                                                op1=ALU.subtract)

            def build_table(m):
                t = table[m]
                for w in range(NQ):
                    dve.wait_ge(transposed, NQ * m + w + 1)
                    dve.tensor_copy(t[:, 0:8, w, :], bank_t(3 * m + w)).then_inc(turned, 1)
                dve.wait_ge(turned, NQ * (m + 1))
                last = None
                for key, s in slots.items():
                    if s < 8:
                        continue
                    if key[0] == "P":
                        last = dve.tensor_scalar(t[:, s], t[:, key[2]], -1.0, None, ALU.mult)
                    else:
                        _, sa, sb_, J = key
                        last = combine(t[:, s], t[:, J], t[:, J + 4], sa, sb_)
                    last.then_inc(slots_built, 1)
                dve.wait_ge(slots_built, (NSLOT - 8) * (m + 1))
                dve.sem_inc(table_ready, 1)

            def down_pieces():
                for (K, p), b in plan.items():
                    rows = slice(NQ * p, NQ * p + NQ)
                    yield rows, 0, K, ("P", *b["P"])
                    for key, src in b["R"]:
                        yield rows, (1 if src >= 4 else 2), K, ("R", *key)

            pieces = list(down_pieces())

            def down_piece(n):
                rows, v, K, key = pieces[n]
                dst = down_w[:, rows, v, K, :]
                if key[0] == "P":
                    ins = dve.tensor_scalar(dst, down_t[:, :, key[2], :], float(key[1]), None, ALU.mult)
                else:
                    _, sa, sb_, J = key
                    ins = combine(dst, down_t[:, :, J, :], down_t[:, :, J + 4, :], sa, sb_)
                ins.then_inc(down_w_ready, 1)

            def y_scale(T):
                dve.wait_ge(y_copied, 4 * (T + 1))
                dve.tensor_reduce(y_max, y_f[:, 0:8, :], AX.XY, ALU.max, apply_absolute_value=True
                                  ).then_inc(y_max_ready, 1)
                dve.tensor_tensor(y_f[:, 8:12, :], y_f[:, 0:4, :], y_f[:, 4:8, :], ALU.add).then_inc(y_summed, 1)

            def y_chain_steps(T):
                dve.wait_ge(y_all_ready, T + 1)
                dve.tensor_scalar(y_all, y_all, 2.0 ** -100, None, ALU.max).then_inc(y_chain, 1)
                dve.wait_ge(y_chain, 6 * T + 1)
                dve.tensor_scalar(y_pow.bitcast(I32), y_all.bitcast(I32), 0x7F800000, None, ALU.bitwise_and
                                  ).then_inc(y_chain, 1)
                dve.wait_ge(y_chain, 6 * T + 2)
                dve.tensor_scalar(y_down, y_pow, 1.0 / TOP, None, ALU.mult).then_inc(y_chain, 1)
                dve.wait_ge(y_chain, 6 * T + 3)
                dve.reciprocal(y_up, y_down).then_inc(y_chain, 1)
                dve.tensor_scalar(gate_scale, y_down, scale[0], None, ALU.mult).then_inc(y_chain, 1)
                dve.tensor_scalar(up_scale, y_down, scale[1], None, ALU.mult).then_inc(y_chain, 1)
                dve.wait_ge(y_chain, 6 * T + 6)

            def y_lo(T):
                dve.wait_ge(y_hi_ready, T + 1)
                dve.scalar_tensor_tensor(out=y_op[:, :, 1, :], in0=y_f[:], scalar=y_up, in1=y_op[:, :, 0, :],
                                         op0=ALU.mult, op1=ALU.subtract).then_inc(y_ready, 1)

            def h_lo(T, c):
                n = NC * T + c
                dve.wait_ge(h_hi_ready, 2 * n + 1)
                dve.scalar_tensor_tensor(out=h_op[:, c, 0:2, 1, :], in0=h_f[:, c], scalar=h_up,
                                         in1=h_op[:, c, 0:2, 0, :], op0=ALU.mult, op1=ALU.subtract
                                         ).then_inc(h_lo_ready, 1)
                dve.wait_ge(h_hi_ready, 2 * n + 2)
                dve.scalar_tensor_tensor(out=h_op[:, c, 2, 1, :], in0=h_sum[:, c % 2, :], scalar=h_up,
                                         in1=h_op[:, c, 2, 0, :], op0=ALU.mult, op1=ALU.subtract
                                         ).then_inc(h_lo_ready, 1)

            def chunk(T, c):
                n = NC * T + c
                dve.wait_ge(products, 3 * n + 2)
                dve.wait_ge(p_copied, n + 1)
                if c >= 2 or not isinstance(T, int) or T > 0:
                    dve.wait_ge(silu_ready, n - 1)
                dve.tensor_tensor(g_sb[:, c % 2], bank_r(c % 2, 0), both(p_sb[:, c % 2, 0:1, :]), ALU.add
                                  ).then_inc(g_ready, 1)
                dve.wait_ge(products, 3 * n + 3)
                dve.tensor_tensor(u_sb[:], bank_r(c % 2, 1), both(p_sb[:, c % 2, 1:2, :]), ALU.add
                                  ).then_inc(u_ready, 1)
                if not isinstance(T, int) or T > 0:
                    h_lo(T - 1, c)
                dve.wait_ge(silu_ready, n + 1)
                dve.wait_ge(u_ready, n + 1)
                if not isinstance(T, int) or T > 0:
                    dve.wait_ge(h_lo_ready, 2 * (NC * (T - 1) + c) + 2)
                dve.scalar_tensor_tensor(out=h_f[:, c], in0=u_sb[:], scalar=up_scale, in1=s_sb[:, c % 2],
                                         op0=ALU.mult, op1=ALU.mult).then_inc(h_ready, 1)
                dve.wait_ge(h_ready, n + 1)
                dve.tensor_reduce(h_max[:, c:c + 1], h_f[:, c], AX.XY, ALU.max, apply_absolute_value=True
                                  ).then_inc(h_max_ready, 1)

            def both(ap):
                return ap.broadcast_to([P, 2, TOK])

            def h_max_all(T):
                dve.wait_ge(h_max_ready, NC * (T + 1))
                dve.tensor_reduce(h_max1, h_max, AX.X, ALU.max).then_inc(h_max1_ready, 1)

            def h_chain_steps(T):
                dve.wait_ge(h_all_ready, T + 1)
                dve.tensor_scalar(h_all, h_all, 2.0 ** -100, None, ALU.max).then_inc(h_chain, 1)
                dve.wait_ge(h_chain, 4 * T + 1)
                dve.tensor_scalar(h_pow.bitcast(I32), h_all.bitcast(I32), 0x7F800000, None, ALU.bitwise_and
                                  ).then_inc(h_chain, 1)
                dve.wait_ge(h_chain, 4 * T + 2)
                dve.tensor_scalar(h_down, h_pow, 1.0 / TOP, None, ALU.mult).then_inc(h_chain, 1)
                dve.wait_ge(h_chain, 4 * T + 3)
                dve.reciprocal(h_up, h_down).then_inc(h_chain, 1)
                dve.wait_ge(h_chain, 4 * T + 4)

            def set_down_scale(T):
                dve.tensor_scalar(down_scale, h_down, scale[2], None, ALU.mult).then_inc(down_scale_ready, 1)

            def add_down(T):
                dve.wait_ge(residual_loaded, 16 * (T + 1))
                dve.wait_ge(down_scale_ready, T + 1)
                for s in range(SUB):
                    n = SUB * T + s
                    dve.wait_ge(down_done, n + 1)
                    for h in range(2):
                        o = o_sb[:, s, HALF * h:HALF * h + HALF]
                        dve.scalar_tensor_tensor(out=o, in0=ps[:, 3 * s + h, :], scalar=down_scale, in1=o,
                                                 op0=ALU.mult, op1=ALU.add).then_inc(r_added, 1)
                    dve.wait_ge(r_added, 2 * (n + 1 + SUB))
                    dve.wait_ge(pd_ready, n + 1 + SUB)
                    o = o_sb[:, s, :].rearrange("p (h o) -> p h o", h=2)
                    pd = pd_sb[:].rearrange("p (a o) -> p a o", a=1).broadcast_to([P, 2, HALF])
                    dve.tensor_tensor(o, o, pd, ALU.add).then_inc(o_ready, 1)

            dve.sem_inc(r_added, 2 * SUB)
            for m in range(2):
                scales(m)
                ternary(m, tern[m], raw[m])
                build_table(m)
                if m == 0:
                    y_scale(0)
            y_chain_steps(0)
            scales(2)
            ternary(2, tern_down, raw_down)
            y_lo(0)
            for w in range(NQ):
                dve.wait_ge(transposed, 2 * NQ + w + 1)
                dve.tensor_copy(down_t[:, w], bank_t(DOWN_BANKS[w])).then_inc(turned, 1)
            dve.wait_ge(turned, 3 * NQ)
            dve.memset(down_t[0:DUP, NQ - 1], 0.0).then_inc(dup_zeroed, 1)
            dve.wait_ge(dup_zeroed, 1)
            per = len(pieces) // NC
            for c in range(NC):
                chunk(0, c)
                for n in range(per * c, per * c + per):
                    down_piece(n)
            dve.wait_ge(down_w_ready, len(pieces))
            h_max_all(0)
            y_scale(1)
            h_chain_steps(0)
            y_chain_steps(1)
            y_lo(1)
            set_down_scale(0)
            with dve.Fori(1, NT - 1) as T:
                for c in range(NC):
                    chunk(T, c)
                h_max_all(T)
                y_scale(T + 1)
                h_chain_steps(T)
                y_chain_steps(T + 1)
                y_lo(T + 1)
                add_down(T - 1)
                set_down_scale(T)
            for c in range(NC):
                chunk(NT - 1, c)
            h_max_all(NT - 1)
            h_chain_steps(NT - 1)
            add_down(NT - 2)
            set_down_scale(NT - 1)
            for c in range(NC):
                h_lo(NT - 1, c)
            add_down(NT - 1)

        @block.tensor
        def _(pe):
            def sum_abs(m):
                pe.wait_ge(abs_summed, min(2 * m + 2, 5))
                pe.wait_ge(consts_set, 4)
                dst = ps[:, TOTAL_BANK[m], 0:1]
                if m < 2:
                    pe.matmul(dst, ones[:], abs_sum[m][:, 0:1], start=True, stop=False)
                    pe.matmul(dst, ones_w2[:], abs_sum[m][:, 1:2], start=False, stop=True
                              ).then_inc(total_ready, 1)
                else:
                    pe.matmul(dst, ones[:], abs_sum[m], start=True, stop=True).then_inc(total_ready, 1)

            def turn(m):
                pe.wait_ge(tern_ready, m + 1)
                if m == 0:
                    pe.wait_ge(ident_set, 1)
                for w in range(NQ):
                    n = 3 * m + w if m < 2 else DOWN_BANKS[w]
                    for j in range(8):
                        src = tern[m][:, w, j, :] if m < 2 else tern_down[:, j, WIN[w]:WIN[w] + P]
                        mm = pe.transpose(bank_t(n)[:, j, :], src, ident[:])
                    mm.then_inc(transposed, 1)

            def y_products(T):
                pe.wait_ge(x_loaded, 16 * (T + 1))
                pe.wait_ge(cond_loaded, 16 * BPT * (T + 1))
                for r in range(4):
                    if r >= 2:
                        pe.wait_ge(y_copied, 4 * T + r - 1)
                    elif not isinstance(T, int) or T > 0:
                        pe.wait_ge(y_copied, 4 * T + r - 1)
                    for i in range(2):
                        for s in range(SUB):
                            f = P * (2 * r + i)
                            mm = pe.matmul(bank_y(r)[:, i, P * s:P * s + P], x_in[:, s, f:f + P],
                                           cond_bd[:, s, :], start=True, stop=True)
                    mm.then_inc(y_done, 1)

            def gate_up(T):
                later = not isinstance(T, int) or T > 0
                pe.wait_ge(y_ready, T + 1)
                for K in range(NP4):
                    for q in range(NQ):
                        c = NQ * K + q
                        s = c % 2
                        n = NC * T + c
                        if later or c >= 2:
                            pe.wait_ge(p_copied, n - 1)
                        if c < 2 and later:
                            pe.wait_ge(pd_ready, SUB * (T - 1) + c + 1)
                        for m in range(2):
                            for p in range(NP4):
                                w = table[m][:, slots["P", *plan[K, p]["P"]], q, :]
                                for e in range(2):
                                    mm = pe.matmul(bank_p(s)[:, m, :], w, y_op[:, 8 + p, e, :],
                                                   start=(p == 0 and e == 0), stop=(p == NP4 - 1 and e == 1))
                        mm.then_inc(products, 1)
                        if c < 2 and later:
                            pe.wait_ge(r_added, 2 * (SUB * (T - 1) + c + 1))
                        for m in range(2):
                            if later or c >= 2:
                                pe.wait_ge(u_ready if m else g_ready, n - 1)
                            for h in range(2):
                                for p in range(NP4):
                                    key, src = plan[K, p]["R"][h]
                                    w = table[m][:, slots["R", *key], q, :]
                                    for e in range(2):
                                        mm = pe.matmul(bank_r(s, m)[:, h, :], w, y_op[:, src, e, :],
                                                       start=(p == 0 and e == 0),
                                                       stop=(p == NP4 - 1 and e == 1))
                            mm.then_inc(products, 1)

            def down(T):
                done = NC * min(T + 2, NT) if isinstance(T, int) else NC * (T + 2)
                for s in range(SUB):
                    pe.wait_ge(p_copied, done - 1 + s)
                    pe.wait_ge(u_ready, done - 1 + s)
                    if isinstance(T, int) and T == NT - 1:
                        pe.wait_ge(pd_ready, SUB * T + s + 1)
                        pe.wait_ge(r_added, 2 * (SUB * T + s + 1))
                    r_bank = [ps[:, 3 * s + h, :].rearrange("p (k o) -> p k o", k=NP4) for h in range(2)]
                    p_bank = ps[:, 3 * s + 2, :].rearrange("p (k o) -> p k o", k=NP4)
                    for p in range(NP4):
                        for q in range(NQ):
                            c = NQ * p + q
                            if s == 0:
                                pe.wait_ge(h_lo_ready, 2 * (NC * T + c + 1))
                            first, last = c == 0, c == NC - 1
                            for e in range(2):
                                st, en = first and e == 0, last and e == 1
                                for v, src in ((0, p), (1, p + 4)):
                                    h_part = h_op[:, c, v, e, P * s:P * s + P]
                                    w = down_w[:, c, 2 - v, :, :]
                                    for h in range(2):
                                        Ks = [K for K in range(NP4) if plan[K, p]["R"][h][1] == src]
                                        if not Ks:
                                            continue
                                        step = Ks[1] - Ks[0]
                                        ks = slice(Ks[0], Ks[-1] + 1, step)
                                        pe.matmul(r_bank[h][:, ks, :], h_part, w[:, ks, :], start=st, stop=en,
                                                  skip_group_check=True)
                                mm = pe.matmul(p_bank, h_op[:, c, 2, e, P * s:P * s + P], down_w[:, c, 0, :, :],
                                               start=st, stop=en)
                    mm.then_inc(down_done, 1)

            sum_abs(0)
            y_products(0)
            turn(0)
            sum_abs(1)
            turn(1)
            pe.wait_ge(turned, 2 * NQ)
            sum_abs(2)
            turn(2)
            pe.wait_ge(turned, 3 * NQ)
            pe.wait_ge(table_ready, 2)
            gate_up(0)
            y_products(1)
            pe.wait_ge(down_w_ready, 3 * len(plan))
            with pe.Fori(1, NT - 1) as T:
                gate_up(T)
                y_products(T + 1)
                down(T - 1)
            gate_up(NT - 1)
            down(NT - 2)
            down(NT - 1)

_INS = ["x", "itok_B_0_15", "L0_cond_weights", "L0_ffn_w_gate", "L0_ffn_w_up", "L0_ffn_w_down"]


def kernel(**inputs):
    import numpy as _np
    import concourse.bacc as _bacc
    from concourse import mybir as _mybir
    from concourse.bass_utils import run_bass_kernel_spmd as _run

    nc = _bacc.Bacc("TRN2", target_bir_lowering=False, num_devices=1)
    arrays, args = {}, []
    for name in _INS:
        a = _np.ascontiguousarray(inputs[name])
        arrays[f"in_{name}_dram"] = a
        args.append(nc.dram_tensor(f"in_{name}_dram", a.shape, _mybir.dt.from_np(a.dtype), kind="ExternalInput").ap())
    args.append(nc.dram_tensor("out_dram", inputs["x"].shape, F32, kind="ExternalOutput").ap())
    build(nc, *args)
    r = _run(nc, [arrays], core_ids=[0])
    return r.results[0]["out_dram"]
```

```python
from contextlib import ExitStack

import concourse.bass as bass
from concourse import mybir

ALU = mybir.AluOpType
ACT = mybir.ActivationFunctionType
F32 = mybir.dt.float32
F16 = mybir.dt.float16
I32 = mybir.dt.int32
AX = mybir.AxisListType

P = 128
TOK = 256
SUB = TOK // P

TRIPLES = [(1, 2, 3), (1, 4, 5), (1, 7, 6), (2, 4, 6), (2, 5, 7), (3, 4, 7), (3, 6, 5)]

GAM = (1, -1, 1, 1)
TAU = (-1, 1, -1, -1)
G2 = (-1, 1)
T2 = (-1, 1)


def octonion_signs():
    s = {(0, 0): 1}
    for i in range(1, 8):
        s[0, i] = 1
        s[i, 0] = 1
        s[i, i] = -1
    for a, b, c in TRIPLES:
        for x, y in ((a, b), (b, c), (c, a)):
            s[x, y] = 1
            s[y, x] = -1
    return [[s[i ^ k, i] for i in range(8)] for k in range(8)]


RHO = (1, 1, 1, 1, 1, 1, 1, -1)
KAPPA = (1, 1, 1, -1, 1, 1, 1, 1)
F_SIGN = {(0, 0): (1, 1, -1, 1), (0, 1): (1, -1, -1, -1), (1, 0): (-1, 1, 1, -1), (1, 1): (1, 1, -1, -1)}


def parity(n):
    return -1 if bin(n).count("1") % 2 else 1


def weight(*terms):
    return tuple(sorted(terms))


def plan():
    e = octonion_signs()
    part, q, pr, r = {}, {}, {}, {}
    for K in range(4):
        for p in range(4):
            a, b, c, d = e[K][p], e[K][p + 4], e[K + 4][p], e[K + 4][p + 4]
            A = K ^ p
            B = A + 4
            if GAM[K] * a * d == TAU[p]:
                part[K, p] = (A, a)
                r[0, K, p] = (weight((B, b), (A, -a * TAU[p])), p + 4)
                r[1, K, p] = (weight((B, c), (A, -a * GAM[K])), p)
            else:
                part[K, p] = (B, b * TAU[p])
                r[0, K, p] = (weight((A, a), (B, -b * TAU[p])), p)
                r[1, K, p] = (weight((A, d), (B, -b * GAM[K])), p + 4)
    for a in range(2):
        for b in range(2):
            X, Y = part[2 * a, 2 * b], part[2 * a, 2 * b + 1]
            Z, W = part[2 * a + 1, 2 * b], part[2 * a + 1, 2 * b + 1]
            if X[0] == W[0] and G2[a] * X[1] * W[1] == T2[b]:
                q[a, b] = weight(X)
                pr[2 * a, b] = (weight(Y, (X[0], -T2[b] * X[1])), 2 * b + 1)
                pr[2 * a + 1, b] = (weight(Z, (X[0], -G2[a] * X[1])), 2 * b)
            else:
                q[a, b] = weight((Y[0], T2[b] * Y[1]))
                pr[2 * a, b] = (weight(X, (Y[0], -T2[b] * Y[1])), 2 * b)
                pr[2 * a + 1, b] = (weight(W, (Y[0], -G2[a] * Y[1])), 2 * b + 1)
    for K in range(4):
        for h in range(2):
            total = {}

            def add(w, f, i):
                for j, s in w:
                    total[j, i] = total.get((j, i), 0) + s * f

            def add_s(w, f, p):
                add(w, f, p)
                add(w, f * TAU[p], p + 4)

            f = GAM[K] if h else 1
            g = G2[K // 2] if K % 2 else 1
            for b in range(2):
                add_s(q[K // 2, b], f * g, 2 * b)
                add_s(q[K // 2, b], f * g * T2[b], 2 * b + 1)
                add_s(pr[K, b][0], f, pr[K, b][1])
            for p in range(4):
                add(*(r[h, K, p][0], 1, r[h, K, p][1]))
            k = K + 4 * h
            assert {x: v for x, v in total.items() if v} == {(i ^ k, i): e[k][i] for i in range(8)}
    return q, pr, r


def down_plan():
    e = octonion_signs()
    corr = {}
    for h in range(2):
        for v in range(2):
            for K in range(4):
                for p in range(4):
                    j = K ^ p
                    given = RHO[K + 4 * h] * KAPPA[p + 4 * v] * F_SIGN[h, v][j] * sum(
                        parity(K & r) * parity(j & r) * parity(p & r) for r in range(4)) // 4
                    if given != e[K + 4 * h][p + 4 * v]:
                        assert (h, v, p) not in corr
                        corr[h, v, p] = (K, weight((j + 4 * (h ^ v), 8 * e[K + 4 * h][p + 4 * v])))
            assert sorted(corr[h, v, p][0] for p in range(4)) == [0, 1, 2, 3]
    return corr


def build(nc, x, cond, cond_w, w_gate, w_up, w_down, out):
    NB, C, D = x.shape
    H8, D8 = w_gate.shape[1], w_gate.shape[2]
    NT = NB * C // TOK
    BPT = TOK // C
    assert D8 == P and D == 8 * P and 2 * C == P and w_down.shape == (8, P, H8)
    WIN = [0, P, H8 - P]
    DUP = 2 * P - WIN[2]
    NQ = len(WIN)
    CHUNKS = [(K, w) for w in range(NQ) for K in range(4)]
    NC = len(CHUNKS)
    NU = NC // 2
    NR = 2 * NQ
    NOP = 14
    HALF = D // 2
    TOP = float(2 ** 12)
    Y_AFTER = {2: 0, 4: 1, 6: 2, 8: 3}
    Y_AFTER_FIRST = {6: 0, 7: 1, 8: 2, 9: 3}
    TURN_AFTER = {1: 0, 3: 1, 5: 2}
    Y_MAX_AFTER, Y_CHAIN_AFTER = 9, 10
    BACK_AFTER = (5, 7)
    G_AFTER = 9
    POOL_SLOTS = 5
    Y_PIECES = [slice(8, 14), slice(0, 4), slice(4, 8)]

    wq, wpr, wr = plan()
    corr = down_plan()
    slots = {weight((j, 1)): j for j in range(8)}
    for w in [*wq.values(), *(v[0] for v in wpr.values()), *(v[0] for v in wr.values())]:
        slots.setdefault(w, len(slots))
    NSLOT = len(slots)

    xr = x.rearrange("b c t -> (b c) t")
    outr = out.rearrange("b c t -> (b c) t")

    with ExitStack() as ctx:
        def sb(name, shape, dt):
            return ctx.enter_context(nc.sbuf_tensor(name, shape, dt))

        def sem(name):
            return ctx.enter_context(nc.semaphore(name))

        table = [sb("gate_table", [P, NSLOT, NQ, P], F16), sb("up_table", [P, NSLOT, NQ, P], F16)]
        down_u = sb("down_u", [P, NQ, 2, 4, 2, P], F16)
        down_c = sb("down_c", [P, NQ, 2, 4, 2, P], F16)
        y_op = sb("y_op", [P, NOP, 2, TOK], F16)
        y_f = sb("y_f", [P, NOP, TOK], F32)
        h_op = sb("h_op", [P, NC, 2, 2, TOK], F16)
        z_op = sb("z_op", [P, NR, 2, 4, TOK], F16)
        h_f = sb("h_f", [P, NC, 2, TOK], F32)
        h_pairs = sb("h_pairs", [P, 2, 2, TOK], F32)
        z_f = sb("z_f", [P, 4, TOK], F32)
        x_in = sb("x_in", [P, SUB, D], F32)
        o_sb = sb("o_sb", [P, SUB, D], F32)
        cond_bd = sb("cond_bd", [P, SUB, P], F32)
        q_sb = sb("q_sb", [P, 2, TOK], F32)
        p_sb = sb("p_sb", [P, 2, TOK], F32)
        g_sb = sb("g_sb", [P, 2, 2, TOK], F32)
        u_sb = sb("u_sb", [P, 2, TOK], F32)
        ud_sb = sb("ud_sb", [P, 2, 2, P], F32)
        wd_sb = sb("wd_sb", [P, 2, 2, 2, P], F32)
        ident = sb("ident", [P, P], F16)
        ones = sb("ones", [P, P], F32)
        ones_w2 = sb("ones_w2", [P, P], F32)
        idx_sb = sb("idx_sb", [1, NB], I32)
        small = sb("small", [P, 64], F32)
        ps = ctx.enter_context(nc.psum_tensor("ps", [P, 8, 512], F32))

        h_op_f32 = h_op[:].rearrange("p a b c t -> p (a b c t)").bitcast(F32)
        z_op_f32 = z_op[:].rearrange("p a b c t -> p (a b c t)").bitcast(F32)
        h_f_flat = h_f[:].rearrange("p a b t -> p (a b t)")
        raw_n = NQ * 8 * P
        raw = [h_op_f32[:, 0:raw_n].rearrange("p (w j d) -> p w j d", w=NQ, j=8),
               h_op_f32[:, raw_n:2 * raw_n].rearrange("p (w j d) -> p w j d", w=NQ, j=8)]
        raw_down = z_op_f32[:, 0:8 * H8].rearrange("p (j d) -> p j d", j=8)
        down_t = h_op_f32[:, 0:raw_n // 2].bitcast(F16).rearrange("p (w j d) -> p w j d", w=NQ, j=8)
        down_pairs = h_op_f32[:, raw_n // 2:raw_n].bitcast(F16).rearrange("p (w j d) -> p w j d", w=NQ, j=8)
        junk = h_f_flat[:, 0:raw_n]
        tern = [h_f_flat[:, raw_n:raw_n + raw_n // 2].bitcast(F16).rearrange("p (w j d) -> p w j d", w=NQ, j=8),
                h_f_flat[:, raw_n + raw_n // 2:2 * raw_n].bitcast(F16).rearrange("p (w j d) -> p w j d", w=NQ, j=8)]
        tern_down = o_sb[:].rearrange("p a t -> p (a t)")[:, 0:4 * H8].bitcast(F16).rearrange(
            "p (j d) -> p j d", j=8)

        def col(n, w=1):
            return small[:, n:n + w]

        abs_sum = [col(0, 3), col(3, 3), col(6)]
        scale = [col(7), col(8), col(9)]
        half = [col(10), col(11), col(12)]
        minus_half = [col(13), col(14), col(15)]
        y_max, y_all, y_pow, y_down, y_up = col(16), col(17), col(18), col(19), col(20)
        gate_scale, up_scale = col(21), col(22)
        h_max1, h_all, h_pow, h_down, h_up, down_scale = col(23), col(24), col(25), col(26), col(27), col(28)
        warm = col(29)
        h_max = col(32, NC)

        Q_BANK, Y_BANK = 6, 7

        def bank_r(s, m):
            return ps[:, 3 * s + m, :].rearrange("p (h t) -> p h t", h=2)

        def bank_pr(s):
            return ps[:, 3 * s + 2, :].rearrange("p (m t) -> p m t", m=2)

        bank_q = ps[:, Q_BANK, :].rearrange("p (m t) -> p m t", m=2)
        def bank_y(T, r):
            n = [Y_BANK, 0, 1, 2][r] if isinstance(T, int) and T == 0 else Y_BANK
            return ps[:, n, :].rearrange("p (i t) -> p i t", i=2)

        total = ps[:, Q_BANK, 0:1]

        def bank_t(n):
            return ps[:, n, :].bitcast(F16).rearrange("p (j d) -> p j d", j=8)

        def down_banks(s):
            return {"c0": ps[:, 3 * s, :].rearrange("p (k o) -> p k o", k=4),
                    "c1": ps[:, 3 * s + 1, :].rearrange("p (k o) -> p k o", k=4),
                    "u0": ps[:, 3 * s + 2, :].rearrange("p (r h o) -> p r h o", r=2, h=2),
                    "u1": ps[:, Q_BANK + s, :].rearrange("p (r h o) -> p r h o", r=2, h=2)}

        gate_loaded = [sem(f"gate_loaded_{w}") for w in range(NQ)]
        up_loaded = sem("up_loaded")
        down_loaded = sem("down_loaded")
        idx_loaded = sem("idx_loaded")
        cond_loaded = sem("cond_loaded")
        x_loaded = sem("x_loaded")
        residual_loaded = sem("residual_loaded")
        out_stored = sem("out_stored")
        ones_set = sem("ones_set")
        ident_set = sem("ident_set")
        cond_zeroed = sem("cond_zeroed")
        abs_summed = sem("abs_summed")
        total_ready = sem("total_ready")
        scale_ready = sem("scale_ready")
        compared = sem("compared")
        tern_ready = sem("tern_ready")
        transposed = sem("transposed")
        turned = sem("turned")
        dup_zeroed = sem("dup_zeroed")
        slots_built = sem("slots_built")
        slots_by_pool = sem("slots_by_pool")
        down_paired = sem("down_paired")
        down_c_ready = sem("down_c_ready")
        down_g_ready = sem("down_g_ready")
        down_g_ready_dve = sem("down_g_ready_dve")
        y_done = sem("y_done")
        y_copied = sem("y_copied")
        y_summed = sem("y_summed")
        y_max_ready = sem("y_max_ready")
        y_all_ready = sem("y_all_ready")
        y_chain = sem("y_chain")
        ffn_scales_set = sem("ffn_scales_set")
        y_hi_ready = sem("y_hi_ready")
        y_ready = sem("y_ready")
        q_done = sem("q_done")
        q_copied = sem("q_copied")
        products = sem("products")
        p_ready = sem("p_ready")
        g_ready = sem("g_ready")
        u_ready = sem("u_ready")
        silu_ready = sem("silu_ready")
        h_ready = sem("h_ready")
        h_max_ready = sem("h_max_ready")
        h_max1_ready = sem("h_max1_ready")
        h_all_ready = sem("h_all_ready")
        reduce_due = sem("reduce_due")
        h_chain = sem("h_chain")
        down_scale_ready = sem("down_scale_ready")
        h_hi_ready = sem("h_hi_ready")
        h_lo_ready = sem("h_lo_ready")
        pairs_ready = sem("pairs_ready")
        z_ready = sem("z_ready")
        z_ready_last = sem("z_ready_last")
        pairs_ready_last = sem("pairs_ready_last")
        z_hi_ready = sem("z_hi_ready")
        z_lo_ready = sem("z_lo_ready")
        down_done = sem("down_done")
        ud_ready = sem("ud_ready")
        wd_ready = sem("wd_ready")
        c_added = sem("c_added")
        w_added = sem("w_added")
        o_ready = sem("o_ready")

        def round_buffer(T, k):
            if isinstance(T, int) and T == NT - 1 and k > 0:
                return x_in[:, k - 1].rearrange("p (r t) -> p r t", r=4) if k < 3 else y_f[:, 4 * k - 12:4 * k - 8]
            return z_f[:]

        def pair_up(eng, add, pairs, k):
            w, v = divmod(k, 2)
            for r0 in range(2):
                signs = [KAPPA[2 * a + 1 + 4 * v] * parity(r0) for a in range(2)]
                a_runs = [(slice(0, 2), signs[0])] if signs[0] == signs[1] else [
                    (slice(a, a + 1), signs[a]) for a in range(2)]
                for a, sign in a_runs:
                    c = 4 * w + 2 * a.start
                    n = a.stop - a.start
                    op = add(pairs[:, a, r0, :], h_f[:, c:c + 2 * n - 1:2, v, :],
                             h_f[:, c + 1:c + 2 * n:2, v, :], sign)
            return op

        def finish_round(add, dst, pairs):
            add(dst[:, 0:2], pairs[:, 0], pairs[:, 1], 1)
            return add(dst[:, 2:4], pairs[:, 0], pairs[:, 1], -1)

        def later(T):
            return not isinstance(T, int) or T > 0

        by_pool = [w for w, n in slots.items() if n >= 8 and len(w) == 2 and w[0][1] > 0][-POOL_SLOTS:]
        DVE_SLOTS = [NSLOT - 8, NSLOT - 8 - len(by_pool)]

        g_blocks = []
        for (h, v), f in F_SIGN.items():
            for r in range(4):
                r1, r0 = divmod(r, 2)
                terms = [(4 * (h ^ v) + 2 * a + (r0 ^ (f[2 * a] != f[2 * a + 1])), f[2 * a] * (1, parity(r1))[a])
                         for a in range(2)]
                g_blocks.append((down_u[:, :, v, r, h, :], tuple(terms)))
        g_of_dve = [b for b in g_blocks if b[1][0][1] < 0 and b[1][1][1] < 0]
        g_of_pool = [b for b in g_blocks if b not in g_of_dve]

        block = ctx.enter_context(nc.Block())

        @block.sync
        def _(sp):
            def load_x(T):
                if later(T):
                    sp.wait_ge(y_done, 4 * T)
                sp.dma_start(x_in[:], xr[bass.ds(T * TOK, TOK), :].rearrange("(s p) t -> p s t", p=P)
                             ).then_inc(x_loaded, 16)

            def load_cond(T):
                for b in range(BPT):
                    h = b % 2
                    which = sp.value_load(idx_sb[0:1, bass.ds(T * BPT + b, 1)], min_val=0,
                                          max_val=cond_w.shape[0] - 1)
                    sp.dma_start(cond_bd[C * h:C * h + C, b // 2, C * h:C * h + C],
                                 cond_w[bass.ds(which, 1), :, :].rearrange("a c d -> (a c) d")
                                 ).then_inc(cond_loaded, 16)

            def load_residual(T):
                if later(T):
                    sp.wait_ge(out_stored, 16 * SUB * T)
                sp.dma_start(o_sb[:], xr[bass.ds(T * TOK, TOK), :].rearrange("(s p) t -> p s t", p=P)
                             ).then_inc(residual_loaded, 16)

            def store(T, s):
                sp.wait_ge(o_ready, SUB * T + s + 2)
                sp.dma_start(outr[bass.ds(T * TOK + s * P, P), :], o_sb[:, s, :]).then_inc(out_stored, 16)

            sp.dma_start(idx_sb[:], cond.rearrange("(a b) -> a b", a=1)).then_inc(idx_loaded, 16)
            for w in range(NQ):
                sp.dma_start(raw[0][:, w], w_gate[:, WIN[w]:WIN[w] + P, :].rearrange("j o d -> o j d")
                             ).then_inc(gate_loaded[w], 16)
            load_x(0)
            sp.wait_ge(idx_loaded, 16)
            sp.wait_ge(cond_zeroed, 1)
            load_cond(0)
            for w in range(NQ):
                sp.dma_start(raw[1][:, w], w_up[:, WIN[w]:WIN[w] + P, :].rearrange("j o d -> o j d")
                             ).then_inc(up_loaded, 16)
            sp.dma_start(raw_down, w_down.rearrange("j o d -> o j d")).then_inc(down_loaded, 16)
            load_x(1)
            load_cond(1)
            sp.wait_ge(transposed, 3 * NQ)
            load_residual(0)
            load_x(2)
            load_cond(2)
            store(0, 0)
            with sp.Fori(2, NT - 1) as T:
                load_x(T + 1)
                load_cond(T + 1)
                store(T - 2, 1)
                load_residual(T - 1)
                store(T - 1, 0)
            store(NT - 3, 1)
            load_residual(NT - 2)
            store(NT - 2, 0)
            store(NT - 2, 1)
            load_residual(NT - 1)
            store(NT - 1, 0)
            store(NT - 1, 1)
            sp.wait_ge(out_stored, 16 * SUB * NT)

        @block.gpsimd
        def _(pool):
            pool.memset(ones[:], 1.0).then_inc(ones_set, 1)
            pool.memset(ones_w2[:], 1.0).then_inc(ones_set, 1)
            pool.memset(ident[:], 0.0).then_inc(ones_set, 1)
            pool.memset(cond_bd[:], 0.0).then_inc(cond_zeroed, 1)
            pool.wait_ge(ones_set, 3)
            pool.memset(ones_w2[0:DUP, :], 0.0).then_inc(ones_set, 1)
            pool.affine_select(out=ident[:], in_=ident[:], compare_op=ALU.not_equal, fill=1.0, base=0,
                               pattern=[[-1, P]], channel_multiplier=1).then_inc(ident_set, 1)

            def signed_add(dst, a, b, sign):
                return pool.tensor_tensor(dst, a, b, ALU.add if sign > 0 else ALU.subtract)

            def all_max(T, own_ready, own, everyone, done):
                pool.wait_ge(own_ready, T + 1)
                pool.sem_inc(reduce_due, 1)
                pool.partition_all_reduce(everyone, own, P, bass.bass_isa.ReduceOp.max).then_inc(done, 1)

            def all_max_h(T):
                all_max(T, h_max1_ready, h_max1, h_all, h_all_ready)

            def all_max_y(T):
                all_max(T, y_max_ready, y_max, y_all, y_all_ready)

            def sum_y(T):
                pool.wait_ge(y_copied, 4 * T + 4)
                if later(T):
                    pool.wait_ge(y_ready, 3 * T)
                for lo, hi in ((0, 1), (1, 2), (2, 4)):
                    signed_add(y_f[:, 8 + lo:8 + hi], y_f[:, lo:hi], y_f[:, 4 + lo:4 + hi], TAU[lo]
                               ).then_inc(y_summed, 1)
                pool.wait_ge(y_summed, 5 * T + 3)
                for b in range(2):
                    signed_add(y_f[:, 12 + b], y_f[:, 8 + 2 * b], y_f[:, 9 + 2 * b], T2[b]
                               ).then_inc(y_summed, 1)
            assert TAU[2] == TAU[3]

            def pairs(T, k):
                pool.wait_ge(h_ready, NC * T + 4 * (k // 2) + 4)
                pool.wait_ge(z_ready, NR * T + k + 1)
                pair_up(pool, signed_add, h_pairs, k).then_inc(pairs_ready, 1)

            def finish(T, k):
                pool.wait_ge(pairs_ready, NR * T + k + 1)
                pool.wait_ge(z_lo_ready, NR * T + k + 1)
                finish_round(signed_add, round_buffer(T, k), h_pairs).then_inc(z_ready, 1)

            def even_rounds_of_last_tile():
                T = NT - 1
                pool.wait_ge(y_done, 4 * NT)
                pool.wait_ge(y_ready, 3 * NT)
                for i, k in enumerate(range(0, NR, 2)):
                    pool.wait_ge(z_ready, NR * T + i + 1)
                    pair_up(pool, signed_add, h_pairs, k).then_inc(pairs_ready, 1)
                    pool.wait_ge(pairs_ready, NR * T + i + 1)
                    if k == 0:
                        pool.wait_ge(z_lo_ready, NR * T + 1)
                    finish_round(signed_add, round_buffer(T, k), h_pairs).then_inc(z_ready, 1)

            def first_rounds(T):
                pairs(T, 0)
                finish(T, 0)
                pairs(T, 1)

            def other_rounds(T):
                for k in range(1, NR):
                    finish(T, k)
                    if k + 1 < NR:
                        pairs(T, k + 1)

            def add_terms(dst, get, w):
                (ja, sa), (jb, sb_) = w
                return signed_add(dst, get(ja), get(jb), sb_) if sa > 0 else signed_add(dst, get(jb), get(ja), -1)

            def up_slots():
                t = table[1]
                pool.wait_ge(turned, 2 * NQ)
                for w in by_pool:
                    add_terms(t[:, slots[w]], lambda j: t[:, j], w).then_inc(slots_by_pool, 1)

            def down_weights():
                pool.wait_ge(turned, 3 * NQ)
                pool.memset(down_t[0:DUP, NQ - 1], 0.0).then_inc(dup_zeroed, 1)
                pool.wait_ge(dup_zeroed, 1)
                for r0 in range(2):
                    signed_add(down_pairs[:, :, r0::2, :], down_t[:, :, 0::2, :], down_t[:, :, 1::2, :],
                               parity(r0)).then_inc(down_paired, 1)
                pool.wait_ge(down_paired, 2)
                for dst, w in g_of_pool:
                    add_terms(dst, lambda j: down_pairs[:, :, j, :], w).then_inc(down_g_ready, 1)

            pool.sem_inc(z_ready, 1)
            all_max_y(0)
            sum_y(0)
            up_slots()
            down_weights()
            sum_y(1)
            all_max_y(1)
            all_max_h(0)
            first_rounds(0)
            with pool.Fori(1, NT - 1) as T:
                other_rounds(T - 1)
                sum_y(T + 1)
                all_max_y(T + 1)
                all_max_h(T)
                first_rounds(T)
            other_rounds(NT - 2)
            all_max_h(NT - 1)
            even_rounds_of_last_tile()

        @block.scalar
        def _(act):
            def copy_y(T, r):
                act.wait_ge(y_done, 4 * T + r + 1)
                if later(T):
                    act.wait_ge(y_ready, 3 * T)
                act.activation(y_f[:, 2 * r:2 * r + 2, :], bank_y(T, r), ACT.Copy).then_inc(y_copied, 1)

            def y_hi(T):
                act.wait_ge(y_chain, 4 * T + 4)
                act.wait_ge(y_summed, 5 * T + 5)
                if later(T):
                    act.wait_ge(products, 3 * NC * T)
                for ops in Y_PIECES:
                    act.activation(y_op[:, ops, 0, :], y_f[:, ops], ACT.Copy, scale=y_up
                                   ).then_inc(y_hi_ready, 1)

            def h_hi(T, c):
                if c == 0:
                    act.wait_ge(h_chain, 4 * (T + 1))
                    act.wait_ge(down_done, SUB * (T + 1))
                act.activation(h_op[:, c, :, 0, :], h_f[:, c], ACT.Copy, scale=h_up).then_inc(h_hi_ready, 1)

            def z_hi(T, k):
                if not (isinstance(T, int) and T == NT - 1):
                    act.wait_ge(z_ready, NR * T + k + 2)
                elif k % 2 == 0:
                    act.wait_ge(z_ready, NR * T + k // 2 + 2)
                else:
                    act.wait_ge(z_ready_last, k // 2 + 1)
                act.activation(z_op[:, k, 0], round_buffer(T, k), ACT.Copy, scale=h_up).then_inc(z_hi_ready, 1)

            def chunk(T, c):
                n, u = NC * T + c, NU * T + c // 2
                if c % 2 == 0:
                    act.wait_ge(q_done, u + 1)
                    if later(T) or c > 0:
                        act.wait_ge(p_ready, n)
                    act.activation(q_sb[:], bank_q, ACT.Copy).then_inc(q_copied, 1)
                if later(T):
                    h_hi(T - 1, c)
                    if c % 2 == 0:
                        z_hi(T - 1, c // 2)
                if c == 0:
                    act.wait_ge(ffn_scales_set, 2 * (T + 1))
                act.wait_ge(g_ready, n + 1)
                act.activation(g_sb[:, c % 2], g_sb[:, c % 2], ACT.Silu, scale=gate_scale
                               ).then_inc(silu_ready, 1)

            def copy_down(T):
                for s in range(SUB):
                    act.wait_ge(down_done, SUB * (T + 1) + s + 1)
                    act.wait_ge(down_scale_ready, T + 1)
                    act.wait_ge(wd_ready, SUB * T + s + SUB)
                    act.activation(ud_sb[:], down_banks(s)["u1"], ACT.Copy, scale=down_scale
                                   ).then_inc(ud_ready, 1)

            def turned_out(n, dst, w):
                act.wait_ge(transposed, n + 1)
                act.activation(dst, bank_t(w), ACT.Copy).then_inc(turned, 1)

            def sum_abs(n, src, size, dst):
                if n > 0:
                    act.wait_ge(abs_summed, n)
                act.activation(junk[:, 0:size], src, ACT.Abs, accum_out=dst).then_inc(abs_summed, 1)

            act.sem_inc(ud_ready, SUB)
            act.wait_ge(ones_set, 1)
            act.activation(warm, ones[:, 0:1], ACT.Silu)
            for w in range(NQ):
                act.wait_ge(gate_loaded[w], 16)
                sum_abs(w, raw[0][:, w].rearrange("p j d -> p (j d)"), 8 * P, abs_sum[0][:, w:w + 1])
            for r in range(4):
                copy_y(0, r)
            act.wait_ge(up_loaded, 16 * NQ)
            for w in range(NQ):
                sum_abs(NQ + w, raw[1][:, w].rearrange("p j d -> p (j d)"), 8 * P, abs_sum[1][:, w:w + 1])
            for w in range(NQ):
                turned_out(w, table[0][:, 0:8, w, :], 3 + w)
            act.wait_ge(down_loaded, 16)
            sum_abs(2 * NQ, raw_down.rearrange("p j d -> p (j d)"), 8 * H8, abs_sum[2])
            for w in range(NQ):
                turned_out(NQ + w, table[1][:, 0:8, w, :], w)
            y_hi(0)
            for c in range(NC):
                chunk(0, c)
                if c in TURN_AFTER:
                    w = TURN_AFTER[c]
                    act.wait_ge(tern_ready, 1)
                    turned_out(2 * NQ + w, down_t[:, w], Y_BANK)
                if c in Y_AFTER_FIRST:
                    copy_y(1, Y_AFTER_FIRST[c])
                if c > max(TURN_AFTER):
                    act.wait_ge(dup_zeroed, 1)
                    n = -(-len(corr) // (NC - max(TURN_AFTER) - 1))
                    i = n * (c - max(TURN_AFTER) - 1)
                    for (h, v, p), (_, w) in list(corr.items())[i:i + n]:
                        (j, eight), = w
                        act.activation(down_c[:, :, v, p, h, :], down_t[:, :, j, :], ACT.Copy, scale=float(eight)
                                       ).then_inc(down_c_ready, 1)
            y_hi(1)
            act.wait_ge(down_c_ready, len(corr))
            act.wait_ge(down_g_ready, len(g_of_pool))
            act.wait_ge(down_g_ready_dve, len(g_of_dve))
            with act.Fori(1, NT - 1) as T:
                for c in range(NC):
                    chunk(T, c)
                    if c in Y_AFTER:
                        copy_y(T + 1, Y_AFTER[c])
                y_hi(T + 1)
                copy_down(T - 1)
            for c in range(NC):
                chunk(NT - 1, c)
            copy_down(NT - 2)
            for w in range(NQ):
                for c in range(4 * w, 4 * w + 4):
                    h_hi(NT - 1, c)
                for k in range(2 * w, 2 * w + 2):
                    z_hi(NT - 1, k)
            copy_down(NT - 1)

        @block.vector
        def _(dve):
            counts = (8 * H8 * P,) * 3

            def signed_add(dst, a, b, sign):
                return dve.tensor_tensor(dst, a, b, ALU.add if sign > 0 else ALU.subtract)

            def scales(m):
                dve.wait_ge(total_ready, m + 1)
                for dst, f in ((scale[m], 1.0), (half[m], 0.5), (minus_half[m], -0.5)):
                    dve.tensor_scalar(dst, total, f / counts[m], None, ALU.mult).then_inc(scale_ready, 1)

            def ternary(m, dst, src, part=0):
                dve.wait_ge(scale_ready, 3 * (m + 1))
                dve.tensor_scalar(dst, src, minus_half[m], None, ALU.is_lt).then_inc(compared, 1)
                dve.wait_ge(compared, m + part + 1)
                dve.scalar_tensor_tensor(out=dst, in0=src, scalar=half[m], in1=dst, op0=ALU.is_gt,
                                         op1=ALU.subtract).then_inc(tern_ready, 1)

            def combine(dst, get, w):
                if len(w) == 1:
                    return dve.tensor_scalar(dst, get(w[0][0]), float(w[0][1]), None, ALU.mult)
                (ja, sa), (jb, sb_) = w
                if sa > 0:
                    return signed_add(dst, get(ja), get(jb), sb_)
                if sb_ > 0:
                    return signed_add(dst, get(jb), get(ja), -1)
                return dve.scalar_tensor_tensor(out=dst, in0=get(ja), scalar=-1.0, in1=get(jb), op0=ALU.mult,
                                                op1=ALU.subtract)

            def build_table(m):
                t = table[m]
                dve.wait_ge(turned, NQ * (m + 1))
                for w, s in slots.items():
                    if s >= 8 and not (m == 1 and w in by_pool):
                        combine(t[:, s], lambda j: t[:, j], w).then_inc(slots_built, 1)

            def y_scale(T):
                dve.wait_ge(y_copied, 4 * T + 4)
                dve.tensor_reduce(y_max, y_f[:, 0:8, :], AX.XY, ALU.max, apply_absolute_value=True
                                  ).then_inc(y_max_ready, 1)

            def power_of_two(T, all_ready, everyone, pow2, down, up, chain):
                dve.wait_ge(all_ready, T + 1)
                dve.tensor_scalar(everyone, everyone, 2.0 ** -100, None, ALU.max).then_inc(chain, 1)
                dve.wait_ge(chain, 4 * T + 1)
                dve.tensor_scalar(pow2.bitcast(I32), everyone.bitcast(I32), 0x7F800000, None, ALU.bitwise_and
                                  ).then_inc(chain, 1)
                dve.wait_ge(chain, 4 * T + 2)
                dve.tensor_scalar(down, pow2, 1.0 / TOP, None, ALU.mult).then_inc(chain, 1)
                dve.wait_ge(chain, 4 * T + 3)
                dve.reciprocal(up, down).then_inc(chain, 1)

            def y_power(T):
                power_of_two(T, y_all_ready, y_all, y_pow, y_down, y_up, y_chain)

            def h_power(T):
                power_of_two(T, h_all_ready, h_all, h_pow, h_down, h_up, h_chain)
                dve.wait_ge(h_chain, 4 * T + 4)

            def ffn_scales(T):
                dve.wait_ge(y_chain, 4 * T + 4)
                if later(T):
                    dve.wait_ge(h_ready, NC * T)
                dve.tensor_scalar(gate_scale, y_down, scale[0], None, ALU.mult).then_inc(ffn_scales_set, 1)
                dve.tensor_scalar(up_scale, y_down, scale[1], None, ALU.mult).then_inc(ffn_scales_set, 1)

            def y_lo(T, pieces):
                dve.wait_ge(y_chain, 4 * T + 4)
                for i in pieces:
                    ops = Y_PIECES[i]
                    dve.wait_ge(y_hi_ready, 3 * T + i + 1)
                    dve.scalar_tensor_tensor(out=y_op[:, ops, 1, :], in0=y_f[:, ops], scalar=y_up,
                                             in1=y_op[:, ops, 0, :], op0=ALU.mult, op1=ALU.subtract
                                             ).then_inc(y_ready, 1)

            def lo_part(dst, src, hi):
                return dve.scalar_tensor_tensor(out=dst, in0=src, scalar=h_up, in1=hi, op0=ALU.mult,
                                                op1=ALU.subtract)

            def h_lo(T, c):
                dve.wait_ge(h_hi_ready, NC * T + c + 1)
                lo_part(h_op[:, c, :, 1, :], h_f[:, c], h_op[:, c, :, 0, :]).then_inc(h_lo_ready, 1)

            def z_lo(T, k):
                dve.wait_ge(z_hi_ready, NR * T + k + 1)
                lo_part(z_op[:, k, 1], round_buffer(T, k), z_op[:, k, 0]).then_inc(z_lo_ready, 1)

            def odd_round_of_last_tile(k):
                i = k // 2
                if i == 0:
                    dve.wait_ge(h_ready, NC * NT)
                    dve.wait_ge(y_done, 4 * NT)
                    dve.wait_ge(y_ready, 3 * NT)
                else:
                    dve.wait_ge(z_ready_last, i)
                pair_up(dve, signed_add, g_sb, k).then_inc(pairs_ready_last, 1)
                dve.wait_ge(pairs_ready_last, i + 1)
                finish_round(signed_add, round_buffer(NT - 1, k), g_sb).then_inc(z_ready_last, 1)

            def add_p(dst, bank, m, K):
                pm = p_sb[:, m:m + 1, :]
                if GAM[K] > 0:
                    return dve.tensor_tensor(dst, bank, pm.broadcast_to([P, 2, TOK]), ALU.add)
                signed_add(dst[:, 0], bank[:, 0], p_sb[:, m], 1)
                return signed_add(dst[:, 1], bank[:, 1], p_sb[:, m], -1)

            def chunk(T, c, with_max):
                n, u = NC * T + c, NU * T + c // 2
                K, s = CHUNKS[c][0], c % 2
                dve.wait_ge(q_copied, u + 1)
                dve.wait_ge(products, 3 * n + 1)
                if c > 0 or later(T):
                    dve.wait_ge(u_ready, n)
                signed_add(p_sb[:], bank_pr(s), q_sb[:], G2[K // 2] if K % 2 else 1).then_inc(p_ready, 1)
                if later(T):
                    h_lo(T - 1, c)
                dve.wait_ge(p_ready, n + 1)
                dve.wait_ge(products, 3 * n + 2)
                if c >= 2 or later(T):
                    dve.wait_ge(h_ready, n - 1)
                add_p(g_sb[:, s], bank_r(s, 0), 0, K).then_inc(g_ready, 1)
                dve.wait_ge(products, 3 * n + 3)
                if c > 0 or later(T):
                    dve.wait_ge(h_ready, n)
                add_p(u_sb[:], bank_r(s, 1), 1, K).then_inc(u_ready, 1)
                if later(T):
                    if c % 2 == 0:
                        z_lo(T - 1, c // 2)
                    dve.wait_ge(h_lo_ready, n - NC + 1)
                    dve.wait_ge(pairs_ready, NR * (T - 1) + 2 * (c // 4) + 2)
                dve.wait_ge(silu_ready, n + 1)
                dve.wait_ge(u_ready, n + 1)
                dve.scalar_tensor_tensor(out=h_f[:, c], in0=u_sb[:], scalar=up_scale, in1=g_sb[:, s],
                                         op0=ALU.mult, op1=ALU.mult).then_inc(h_ready, 1)
                if with_max:
                    dve.wait_ge(h_ready, n + 1)
                    dve.tensor_reduce(h_max[:, c:c + 1], h_f[:, c], AX.XY, ALU.max, apply_absolute_value=True
                                      ).then_inc(h_max_ready, 1)

            def h_max_of_chunks(tiles):
                dve.wait_ge(h_max_ready, NC * tiles)
                dve.tensor_reduce(h_max1, h_max, AX.X, ALU.max).then_inc(h_max1_ready, 1)

            def h_max_of_tile(T):
                dve.wait_ge(h_ready, NC * (T + 1))
                dve.tensor_reduce(h_max1, h_f[:], AX.XYZ, ALU.max, apply_absolute_value=True
                                  ).then_inc(h_max1_ready, 1)

            def set_down_scale(T):
                if later(T):
                    dve.wait_ge(wd_ready, SUB * (T + 1))
                dve.tensor_scalar(down_scale, h_down, scale[2], 0.25, ALU.mult, ALU.mult).then_inc(down_scale_ready, 1)

            def add_down(T, s):
                n = SUB * T + s
                banks = down_banks(s)
                if s == 0:
                    dve.wait_ge(residual_loaded, 16 * (T + 1))
                    dve.wait_ge(down_scale_ready, T + 1)
                dve.wait_ge(down_done, n + SUB + 1)
                o = o_sb[:, s, :].rearrange("p (h k o) -> p h k o", h=2, k=4)
                for h in range(2):
                    last = dve.scalar_tensor_tensor(out=o[:, h], in0=banks[f"c{h}"], scalar=down_scale,
                                                    in1=o[:, h], op0=ALU.mult, op1=ALU.add)
                last.then_inc(c_added, 1)
                dve.wait_ge(ud_ready, n + SUB + 1)
                dve.wait_ge(o_ready, n + 1)
                for k1 in range(2):
                    last = dve.scalar_tensor_tensor(out=wd_sb[:, k1], in0=banks["u0"], scalar=down_scale,
                                                    in1=ud_sb[:], op0=ALU.mult,
                                                    op1=ALU.subtract if k1 else ALU.add)
                last.then_inc(wd_ready, 1)

            def back_to_outputs(T, s, r0):
                n = SUB * T + s
                if r0 == 0:
                    dve.wait_ge(c_added, n + SUB + 1)
                    dve.wait_ge(wd_ready, n + SUB + 1)
                else:
                    dve.wait_ge(w_added, n + 1)
                o = o_sb[:, s, :].rearrange("p (h a b o) -> p h a b o", h=2, a=2, b=2)
                for h in range(2):
                    for k0 in range(2):
                        signs = [RHO[4 * h + 2 * k1 + k0] * parity(k0 & r0) for k1 in range(2)]
                        k1_runs = [(slice(0, 2), signs[0])] if signs[0] == signs[1] else [
                            (slice(k1, k1 + 1), signs[k1]) for k1 in range(2)]
                        for k1, sign in k1_runs:
                            dst = o[:, h, k1, k0, :]
                            last = signed_add(dst, dst, wd_sb[:, k1, r0, h, :], sign)
                last.then_inc(o_ready if r0 else w_added, 1)

            dve.sem_inc(wd_ready, SUB)
            dve.sem_inc(c_added, SUB)
            dve.sem_inc(z_lo_ready, 1)
            dve.sem_inc(o_ready, 1)
            scales(0)
            ternary(0, tern[0], raw[0])
            y_scale(0)
            scales(1)
            ternary(1, tern[1], raw[1])
            y_power(0)
            ffn_scales(0)
            scales(2)
            build_table(0)
            y_lo(0, range(0, 1))
            build_table(1)
            y_lo(0, range(1, len(Y_PIECES)))
            for c in range(NC):
                chunk(0, c, with_max=True)
                if c < NQ:
                    part = slice(P * c, min(P * c + P, H8))
                    ternary(2, tern_down[:, :, part], raw_down[:, :, part], c)
                if c == G_AFTER:
                    dve.wait_ge(down_paired, 2)
                    for dst, w in g_of_dve:
                        combine(dst, lambda j: down_pairs[:, :, j, :], w).then_inc(down_g_ready_dve, 1)
                if c == Y_MAX_AFTER:
                    y_scale(1)
                if c == Y_CHAIN_AFTER:
                    y_power(1)
            ffn_scales(1)
            h_max_of_chunks(1)
            y_lo(1, range(len(Y_PIECES)))
            h_power(0)
            set_down_scale(0)

            def tile(T):
                for c in range(NC):
                    chunk(T, c, with_max=False)
                    if c in BACK_AFTER and (not isinstance(T, int) or T > 1):
                        back_to_outputs(T - 2, SUB - 1, BACK_AFTER.index(c))
                    if c == Y_MAX_AFTER:
                        y_scale(T + 1)
                    if c == Y_CHAIN_AFTER:
                        y_power(T + 1)
                ffn_scales(T + 1)
                y_lo(T + 1, range(len(Y_PIECES)))
                h_max_of_tile(T)
                h_power(T)
                add_down(T - 1, 0)
                for r0 in range(2):
                    back_to_outputs(T - 1, 0, r0)
                add_down(T - 1, 1)
                set_down_scale(T)

            tile(1)
            with dve.Fori(2, NT - 1) as T:
                tile(T)
            for c in range(NC):
                chunk(NT - 1, c, with_max=True)
                if c in BACK_AFTER:
                    back_to_outputs(NT - 3, SUB - 1, BACK_AFTER.index(c))
            h_max_of_chunks(2)
            odd_round_of_last_tile(1)
            h_power(NT - 1)
            for k in range(3, NR, 2):
                odd_round_of_last_tile(k)
            for s in range(SUB):
                add_down(NT - 2, s)
                for r0 in range(2):
                    back_to_outputs(NT - 2, s, r0)
            set_down_scale(NT - 1)
            for w in range(NQ):
                for c in range(4 * w, 4 * w + 4):
                    h_lo(NT - 1, c)
                for k in range(2 * w, 2 * w + 2):
                    z_lo(NT - 1, k)
            for s in range(SUB):
                add_down(NT - 1, s)
                for r0 in range(2):
                    back_to_outputs(NT - 1, s, r0)

        @block.tensor
        def _(pe):
            def sum_abs(m):
                pe.wait_ge(abs_summed, min(3 * m + 3, 7))
                if m < 2:
                    for w in range(NQ):
                        mm = pe.matmul(total, (ones_w2 if w == NQ - 1 else ones)[:], abs_sum[m][:, w:w + 1],
                                       start=(w == 0), stop=(w == NQ - 1))
                else:
                    mm = pe.matmul(total, ones[:], abs_sum[m], start=True, stop=True)
                mm.then_inc(total_ready, 1)

            def turn(m, w, bank):
                pe.wait_ge(tern_ready, m + 1 if m < 2 else 3 + w)
                for j in range(8):
                    src = tern[m][:, w, j, :] if m < 2 else tern_down[:, j, WIN[w]:WIN[w] + P]
                    mm = pe.transpose(bank_t(bank)[:, j, :], src, ident[:])
                mm.then_inc(transposed, 1)

            def y_round(T, r):
                if r == 0:
                    pe.wait_ge(x_loaded, 16 * (T + 1))
                    pe.wait_ge(cond_loaded, 16 * BPT * (T + 1))
                if later(T):
                    pe.wait_ge(y_copied, 4 * T + r)
                for i in range(2):
                    for s in range(SUB):
                        f = P * (2 * r + i)
                        mm = pe.matmul(bank_y(T, r)[:, i, P * s:P * s + P], x_in[:, s, f:f + P], cond_bd[:, s, :],
                                       start=True, stop=True)
                mm.then_inc(y_done, 1)

            def group(dst, m, terms):
                for i, (slot, q, op) in enumerate(terms):
                    for e in range(2):
                        mm = pe.matmul(dst, table[m][:, slot, q, :], y_op[:, op, e, :],
                                       start=(i == 0 and e == 0), stop=(i == len(terms) - 1 and e == 1))
                return mm

            def gate_up(T, c):
                K, q = CHUNKS[c]
                s, n, u = c % 2, NC * T + c, NU * T + c // 2
                if c == 0:
                    pe.wait_ge(y_ready, 3 * T + 1)
                if c % 2 == 0:
                    if later(T) or c > 0:
                        pe.wait_ge(q_copied, u)
                    if c == 0 and later(T):
                        pe.wait_ge(ud_ready, SUB * (T - 1) + 1)
                    for m in range(2):
                        if m == 1 and c == 0 and not later(T):
                            pe.wait_ge(slots_built, sum(DVE_SLOTS))
                            pe.wait_ge(slots_by_pool, len(by_pool))
                        mm = group(bank_q[:, m], m, [(slots[wq[K // 2, b]], q, 12 + b) for b in range(2)])
                    mm.then_inc(q_done, 1)
                if c >= 2 or later(T):
                    pe.wait_ge(p_ready, n - 1)
                if c < 2 and later(T):
                    pe.wait_ge(wd_ready, SUB * (T - 1) + c + 1)
                for m in range(2):
                    mm = group(bank_pr(s)[:, m], m, [(slots[wpr[K, b][0]], q, 8 + wpr[K, b][1]) for b in range(2)])
                mm.then_inc(products, 1)
                if c == 0:
                    pe.wait_ge(y_ready, 3 * T + 3)
                if c < 2 and later(T):
                    pe.wait_ge(c_added, SUB * (T - 1) + c + 1)
                for m in range(2):
                    if c >= 2 or later(T):
                        pe.wait_ge(u_ready if m else g_ready, n - 1)
                    for h in range(2):
                        mm = group(bank_r(s, m)[:, h], m, [(slots[wr[h, K, p][0]], q, wr[h, K, p][1])
                                                           for p in range(4)])
                    mm.then_inc(products, 1)

            def down_products():
                for w in range(NQ):
                    for p in range(4):
                        for v in range(2):
                            for e in range(2):
                                for h in range(2):
                                    yield (2 * w + p // 2, False, f"c{h}", corr[h, v, p][0],
                                           h_op[:, 4 * w + p, v, e], down_c[:, w, v, p, h])
                    for v in range(2):
                        for e in range(2):
                            for r in range(4):
                                yield (2 * w + v, True, f"u{r // 2}", r % 2, z_op[:, 2 * w + v, e, r],
                                       down_u[:, w, v, r])

            products_of_down = list(down_products())
            first = {bank: next(i for i, x in enumerate(products_of_down) if x[2] == bank)
                     for bank in ("c0", "c1", "u0", "u1")}
            last = {x[2]: i for i, x in enumerate(products_of_down)}

            def down(T):
                done = NC * (T + 2) if not isinstance(T, int) else NC * min(T + 2, NT)
                for s in range(SUB):
                    banks = down_banks(s)
                    pe.wait_ge(u_ready, done - 1 + s)
                    if isinstance(T, int) and T == NT - 1:
                        pe.wait_ge(wd_ready, SUB * T + s + 1)
                        pe.wait_ge(ud_ready, SUB * T + s + 1)
                        pe.wait_ge(c_added, SUB * T + s + 1)
                    got = None
                    for i, (k, is_z, bank, place, operand, w) in enumerate(products_of_down):
                        if s == 0 and (k, is_z) != got:
                            got = (k, is_z)
                            if is_z:
                                pe.wait_ge(z_lo_ready, NR * T + k + 2)
                            else:
                                pe.wait_ge(h_lo_ready, NC * T + 2 * k + 2)
                        mm = pe.matmul(banks[bank][:, place], operand[:, P * s:P * s + P], w,
                                       start=(i == first[bank]), stop=(i == last[bank]), skip_group_check=True)
                    mm.then_inc(down_done, 1)

            pe.sem_inc(down_done, SUB)
            pe.wait_ge(ones_set, 4)
            pe.wait_ge(ident_set, 1)
            sum_abs(0)
            for r in range(4):
                y_round(0, r)
            for w in range(NQ):
                turn(0, w, 3 + w)
            pe.wait_ge(scale_ready, 3)
            sum_abs(1)
            pe.wait_ge(scale_ready, 6)
            sum_abs(2)
            pe.wait_ge(y_copied, 4)
            for w in range(NQ):
                turn(1, w, w)
            pe.wait_ge(turned, 2 * NQ)
            pe.wait_ge(slots_built, DVE_SLOTS[0])
            pe.wait_ge(scale_ready, 9)
            for c in range(NC):
                gate_up(0, c)
                if c in TURN_AFTER:
                    w = TURN_AFTER[c]
                    pe.wait_ge(y_copied, 4)
                    pe.wait_ge(turned, 2 * NQ + w)
                    turn(2, w, Y_BANK)
                if c in Y_AFTER_FIRST:
                    pe.wait_ge(turned, 3 * NQ)
                    y_round(1, Y_AFTER_FIRST[c])
            pe.wait_ge(down_c_ready, len(corr))
            pe.wait_ge(down_g_ready, len(g_of_pool))
            pe.wait_ge(down_g_ready_dve, len(g_of_dve))
            with pe.Fori(1, NT - 1) as T:
                for c in range(NC):
                    gate_up(T, c)
                    if c in Y_AFTER:
                        if Y_AFTER[c] == 0:
                            pe.wait_ge(ud_ready, SUB * T)
                        y_round(T + 1, Y_AFTER[c])
                pe.wait_ge(y_copied, 4 * (T + 2))
                down(T - 1)
            for c in range(NC):
                gate_up(NT - 1, c)
            down(NT - 2)
            down(NT - 1)


_INS = ["x", "itok_B_0_15", "L0_cond_weights", "L0_ffn_w_gate", "L0_ffn_w_up", "L0_ffn_w_down"]


def kernel(**inputs):
    import numpy as _np
    import concourse.bacc as _bacc
    from concourse import mybir as _mybir
    from concourse.bass_utils import run_bass_kernel_spmd as _run

    nc = _bacc.Bacc("TRN2", target_bir_lowering=False, num_devices=1)
    arrays, args = {}, []
    for name in _INS:
        a = _np.ascontiguousarray(inputs[name])
        arrays[f"in_{name}_dram"] = a
        args.append(nc.dram_tensor(f"in_{name}_dram", a.shape, _mybir.dt.from_np(a.dtype), kind="ExternalInput").ap())
    args.append(nc.dram_tensor("out_dram", inputs["x"].shape, F32, kind="ExternalOutput").ap())
    build(nc, *args)
    r = _run(nc, [arrays], core_ids=[0])
    return r.results[0]["out_dram"]
```

```python
from contextlib import ExitStack

import concourse.bass as bass
from concourse import mybir

ALU = mybir.AluOpType
ACT = mybir.ActivationFunctionType
F32 = mybir.dt.float32
F16 = mybir.dt.float16
I32 = mybir.dt.int32
AX = mybir.AxisListType

P = 128
TOK = 256
SUB = TOK // P

TRIPLES = [(1, 2, 3), (1, 4, 5), (1, 7, 6), (2, 4, 6), (2, 5, 7), (3, 4, 7), (3, 6, 5)]

GAM = (1, -1, 1, 1)
TAU = (-1, 1, -1, -1)
G2 = (-1, 1)
T2 = (-1, 1)


def octonion_signs():
    s = {(0, 0): 1}
    for i in range(1, 8):
        s[0, i] = 1
        s[i, 0] = 1
        s[i, i] = -1
    for a, b, c in TRIPLES:
        for x, y in ((a, b), (b, c), (c, a)):
            s[x, y] = 1
            s[y, x] = -1
    return [[s[i ^ k, i] for i in range(8)] for k in range(8)]


RHO = (1, 1, 1, 1, 1, 1, 1, -1)
KAPPA = (1, 1, 1, -1, 1, 1, 1, 1)
F_SIGN = {(0, 0): (1, 1, -1, 1), (0, 1): (1, -1, -1, -1), (1, 0): (-1, 1, 1, -1), (1, 1): (1, 1, -1, -1)}


def parity(n):
    return -1 if bin(n).count("1") % 2 else 1


def weight(*terms):
    return tuple(sorted(terms))


def plan():
    e = octonion_signs()
    part, q, pr, r = {}, {}, {}, {}
    for K in range(4):
        for p in range(4):
            a, b, c, d = e[K][p], e[K][p + 4], e[K + 4][p], e[K + 4][p + 4]
            A = K ^ p
            B = A + 4
            if GAM[K] * a * d == TAU[p]:
                part[K, p] = (A, a)
                r[0, K, p] = (weight((B, b), (A, -a * TAU[p])), p + 4)
                r[1, K, p] = (weight((B, c), (A, -a * GAM[K])), p)
            else:
                part[K, p] = (B, b * TAU[p])
                r[0, K, p] = (weight((A, a), (B, -b * TAU[p])), p)
                r[1, K, p] = (weight((A, d), (B, -b * GAM[K])), p + 4)
    for a in range(2):
        for b in range(2):
            X, Y = part[2 * a, 2 * b], part[2 * a, 2 * b + 1]
            Z, W = part[2 * a + 1, 2 * b], part[2 * a + 1, 2 * b + 1]
            if X[0] == W[0] and G2[a] * X[1] * W[1] == T2[b]:
                q[a, b] = weight(X)
                pr[2 * a, b] = (weight(Y, (X[0], -T2[b] * X[1])), 2 * b + 1)
                pr[2 * a + 1, b] = (weight(Z, (X[0], -G2[a] * X[1])), 2 * b)
            else:
                q[a, b] = weight((Y[0], T2[b] * Y[1]))
                pr[2 * a, b] = (weight(X, (Y[0], -T2[b] * Y[1])), 2 * b)
                pr[2 * a + 1, b] = (weight(W, (Y[0], -G2[a] * Y[1])), 2 * b + 1)
    for K in range(4):
        for h in range(2):
            total = {}

            def add(w, f, i):
                for j, s in w:
                    total[j, i] = total.get((j, i), 0) + s * f

            def add_s(w, f, p):
                add(w, f, p)
                add(w, f * TAU[p], p + 4)

            f = GAM[K] if h else 1
            g = G2[K // 2] if K % 2 else 1
            for b in range(2):
                add_s(q[K // 2, b], f * g, 2 * b)
                add_s(q[K // 2, b], f * g * T2[b], 2 * b + 1)
                add_s(pr[K, b][0], f, pr[K, b][1])
            for p in range(4):
                add(*(r[h, K, p][0], 1, r[h, K, p][1]))
            k = K + 4 * h
            assert {x: v for x, v in total.items() if v} == {(i ^ k, i): e[k][i] for i in range(8)}
    return q, pr, r


def down_plan():
    e = octonion_signs()
    corr = {}
    for h in range(2):
        for v in range(2):
            for K in range(4):
                for p in range(4):
                    j = K ^ p
                    given = RHO[K + 4 * h] * KAPPA[p + 4 * v] * F_SIGN[h, v][j] * sum(
                        parity(K & r) * parity(j & r) * parity(p & r) for r in range(4)) // 4
                    if given != e[K + 4 * h][p + 4 * v]:
                        assert (h, v, p) not in corr
                        corr[h, v, p] = (K, weight((j + 4 * (h ^ v), 8 * e[K + 4 * h][p + 4 * v])))
            assert sorted(corr[h, v, p][0] for p in range(4)) == [0, 1, 2, 3]
    return corr


def build(nc, x, cond, cond_w, w_gate, w_up, w_down, out):
    NB, C, D = x.shape
    H8, D8 = w_gate.shape[1], w_gate.shape[2]
    NT = NB * C // TOK
    BPT = TOK // C
    assert D8 == P and D == 8 * P and 2 * C == P and w_down.shape == (8, P, H8)
    WIN = [0, P, H8 - P]
    DUP = 2 * P - WIN[2]
    NQ = len(WIN)
    CHUNKS = [(K, w) for w in range(NQ) for K in range(4)]
    NC = len(CHUNKS)
    NU = NC // 2
    NR = 2 * NQ
    NOP = 14
    HALF = D // 2
    TOP = float(2 ** 12)
    Y_AFTER = {2: 0, 4: 1, 6: 2, 8: 3}
    Y_AFTER_FIRST = {6: (0,), 7: (1,), 8: (2, 3)}
    TURN_AFTER = {1: 0, 3: 1, 5: 2}
    Y_MAX_AFTER, Y_CHAIN_AFTER = 9, 10
    BACK_AFTER = (5, 7)
    LAST_OF_DVE = (1, 3)
    LAST_OF_POOL = tuple(k for k in range(NR) if k not in LAST_OF_DVE)
    G_AFTER = 9
    POOL_SLOTS = (6, 8)
    Y_PIECES = [slice(8, 14), slice(0, 4), slice(4, 8)]

    wq, wpr, wr = plan()
    corr = down_plan()
    slots = {weight((j, 1)): j for j in range(8)}
    for w in [*wq.values(), *(v[0] for v in wpr.values()), *(v[0] for v in wr.values())]:
        slots.setdefault(w, len(slots))
    NSLOT = len(slots)

    xr = x.rearrange("b c t -> (b c) t")
    outr = out.rearrange("b c t -> (b c) t")

    with ExitStack() as ctx:
        def sb(name, shape, dt):
            return ctx.enter_context(nc.sbuf_tensor(name, shape, dt))

        def sem(name):
            return ctx.enter_context(nc.semaphore(name))

        table = [sb("gate_table", [P, NSLOT, NQ, P], F16), sb("up_table", [P, NSLOT, NQ, P], F16)]
        down_u = sb("down_u", [P, NQ, 2, 4, 2, P], F16)
        down_c = sb("down_c", [P, NQ, 2, 4, 2, P], F16)
        y_op = sb("y_op", [P, NOP, 2, TOK], F16)
        y_f = sb("y_f", [P, NOP, TOK], F32)
        h_op = sb("h_op", [P, NC, 2, 2, TOK], F16)
        z_op = sb("z_op", [P, NR, 2, 4, TOK], F16)
        h_f = sb("h_f", [P, NC, 2, TOK], F32)
        h_pairs = sb("h_pairs", [P, 2, 2, TOK], F32)
        z_f = sb("z_f", [P, 4, TOK], F32)
        x_in = sb("x_in", [P, SUB, D], F32)
        o_sb = sb("o_sb", [P, SUB, D], F32)
        cond_bd = sb("cond_bd", [P, SUB, P], F32)
        q_sb = sb("q_sb", [P, 2, TOK], F32)
        p_sb = sb("p_sb", [P, 2, TOK], F32)
        g_sb = sb("g_sb", [P, 2, 2, TOK], F32)
        u_sb = sb("u_sb", [P, 2, TOK], F32)
        ud_sb = sb("ud_sb", [P, 2, 2, P], F32)
        wd_sb = sb("wd_sb", [P, 2, 2, 2, P], F32)
        ident = sb("ident", [P, P], F16)
        ones = sb("ones", [P, P], F32)
        ones_w2 = sb("ones_w2", [P, P], F32)
        idx_sb = sb("idx_sb", [1, NB], I32)
        small = sb("small", [P, 64], F32)
        ps = ctx.enter_context(nc.psum_tensor("ps", [P, 8, 512], F32))

        h_op_f32 = h_op[:].rearrange("p a b c t -> p (a b c t)").bitcast(F32)
        z_op_f32 = z_op[:].rearrange("p a b c t -> p (a b c t)").bitcast(F32)
        h_f_flat = h_f[:].rearrange("p a b t -> p (a b t)")
        raw_n = NQ * 8 * P
        raw = [h_op_f32[:, 0:raw_n].rearrange("p (w j d) -> p w j d", w=NQ, j=8),
               h_op_f32[:, raw_n:2 * raw_n].rearrange("p (w j d) -> p w j d", w=NQ, j=8)]
        raw_down = z_op_f32[:, 0:8 * H8].rearrange("p (j d) -> p j d", j=8)
        down_t = h_op_f32[:, 0:raw_n // 2].bitcast(F16).rearrange("p (w j d) -> p w j d", w=NQ, j=8)
        down_pairs = h_op_f32[:, raw_n // 2:raw_n].bitcast(F16).rearrange("p (w j d) -> p w j d", w=NQ, j=8)
        junk = h_f_flat[:, 0:raw_n]
        tern = [h_f_flat[:, raw_n:raw_n + raw_n // 2].bitcast(F16).rearrange("p (w j d) -> p w j d", w=NQ, j=8),
                h_f_flat[:, raw_n + raw_n // 2:2 * raw_n].bitcast(F16).rearrange("p (w j d) -> p w j d", w=NQ, j=8)]
        tern_down = o_sb[:].rearrange("p a t -> p (a t)")[:, 0:4 * H8].bitcast(F16).rearrange(
            "p (j d) -> p j d", j=8)

        def col(n, w=1):
            return small[:, n:n + w]

        abs_sum = [col(0, 3), col(3, 3), col(6)]
        scale = [col(7), col(8), col(9)]
        half = [col(10), col(11), col(12)]
        minus_half = [col(13), col(14), col(15)]
        y_max, y_all, y_pow, y_down, y_up = col(16), col(17), col(18), col(19), col(20)
        gate_scale, up_scale = col(21), col(22)
        h_max1, h_all, h_pow, h_down, h_up, down_scale = col(23), col(24), col(25), col(26), col(27), col(28)
        warm = col(29)
        h_max = col(32, NC)

        Q_BANK, Y_BANK = 6, 7

        def bank_r(s, m):
            return ps[:, 3 * s + m, :].rearrange("p (h t) -> p h t", h=2)

        def bank_pr(s):
            return ps[:, 3 * s + 2, :].rearrange("p (m t) -> p m t", m=2)

        bank_q = ps[:, Q_BANK, :].rearrange("p (m t) -> p m t", m=2)
        def bank_y(T, r):
            n = [Y_BANK, 0, 1, 2][r] if isinstance(T, int) and T == 0 else Y_BANK
            return ps[:, n, :].rearrange("p (i t) -> p i t", i=2)

        total = ps[:, Q_BANK, 0:1]

        def bank_t(n):
            return ps[:, n, :].bitcast(F16).rearrange("p (j d) -> p j d", j=8)

        def down_banks(s):
            return {"c0": ps[:, 3 * s, :].rearrange("p (k o) -> p k o", k=4),
                    "c1": ps[:, 3 * s + 1, :].rearrange("p (k o) -> p k o", k=4),
                    "u0": ps[:, 3 * s + 2, :].rearrange("p (r h o) -> p r h o", r=2, h=2),
                    "u1": ps[:, Q_BANK + s, :].rearrange("p (r h o) -> p r h o", r=2, h=2)}

        gate_loaded = [sem(f"gate_loaded_{w}") for w in range(NQ)]
        up_loaded = [sem(f"up_loaded_{w}") for w in range(NQ)]
        down_loaded = sem("down_loaded")
        idx_loaded = sem("idx_loaded")
        cond_loaded = sem("cond_loaded")
        x_loaded = sem("x_loaded")
        residual_loaded = sem("residual_loaded")
        out_stored = sem("out_stored")
        ones_set = sem("ones_set")
        ident_set = sem("ident_set")
        cond_zeroed = sem("cond_zeroed")
        abs_summed = sem("abs_summed")
        total_ready = sem("total_ready")
        scale_ready = sem("scale_ready")
        compared = sem("compared")
        tern_ready = sem("tern_ready")
        transposed = sem("transposed")
        turned = sem("turned")
        dup_zeroed = sem("dup_zeroed")
        slots_built = sem("slots_built")
        slots_by_pool = sem("slots_by_pool")
        down_paired = sem("down_paired")
        down_c_ready = sem("down_c_ready")
        down_g_ready = sem("down_g_ready")
        down_g_ready_dve = sem("down_g_ready_dve")
        y_done = sem("y_done")
        y_copied = sem("y_copied")
        y_summed = sem("y_summed")
        y_max_ready = sem("y_max_ready")
        y_all_ready = sem("y_all_ready")
        y_chain = sem("y_chain")
        ffn_scales_set = sem("ffn_scales_set")
        y_hi_ready = sem("y_hi_ready")
        y_ready = sem("y_ready")
        q_done = sem("q_done")
        q_copied = sem("q_copied")
        products = sem("products")
        p_ready = sem("p_ready")
        g_ready = sem("g_ready")
        u_ready = sem("u_ready")
        silu_ready = sem("silu_ready")
        h_ready = sem("h_ready")
        h_max_ready = sem("h_max_ready")
        h_max1_ready = sem("h_max1_ready")
        h_all_ready = sem("h_all_ready")
        reduce_due = sem("reduce_due")
        h_chain = sem("h_chain")
        down_scale_ready = sem("down_scale_ready")
        h_hi_ready = sem("h_hi_ready")
        h_lo_ready = sem("h_lo_ready")
        pairs_ready = sem("pairs_ready")
        z_ready = sem("z_ready")
        z_ready_last = sem("z_ready_last")
        pairs_ready_last = sem("pairs_ready_last")
        z_hi_ready = sem("z_hi_ready")
        z_lo_ready = sem("z_lo_ready")
        parts_read = sem("parts_read")
        last_c_done = sem("last_c_done")
        last_u1_done = sem("last_u1_done")
        down_done = sem("down_done")
        ud_ready = sem("ud_ready")
        wd_ready = sem("wd_ready")
        c_added = sem("c_added")
        w_added = sem("w_added")
        o_ready = sem("o_ready")

        def rows_of(T):
            if isinstance(T, int) and T == NT - 1:
                return h_f_flat[:, 0:SUB * D].rearrange("p (s t) -> p s t", s=SUB)
            return o_sb[:]

        def wd_of(T, s):
            if isinstance(T, int) and (T, s) == (NT - 2, SUB - 1):
                return g_sb[:].rearrange("p a r (h o) -> p a r h o", h=2)
            return wd_sb[:]

        def round_buffer(T, k):
            if isinstance(T, int) and T == NT - 1 and k > 0:
                return x_in[:, k - 1].rearrange("p (r t) -> p r t", r=4) if k < 3 else y_f[:, 4 * k - 12:4 * k - 8]
            return z_f[:]

        def pair_up(eng, add, pairs, k):
            w, v = divmod(k, 2)
            for r0 in range(2):
                signs = [KAPPA[2 * a + 1 + 4 * v] * parity(r0) for a in range(2)]
                a_runs = [(slice(0, 2), signs[0])] if signs[0] == signs[1] else [
                    (slice(a, a + 1), signs[a]) for a in range(2)]
                for a, sign in a_runs:
                    c = 4 * w + 2 * a.start
                    n = a.stop - a.start
                    op = add(pairs[:, a, r0, :], h_f[:, c:c + 2 * n - 1:2, v, :],
                             h_f[:, c + 1:c + 2 * n:2, v, :], sign)
            return op

        def finish_round(add, dst, pairs):
            add(dst[:, 0:2], pairs[:, 0], pairs[:, 1], 1)
            return add(dst[:, 2:4], pairs[:, 0], pairs[:, 1], -1)

        def later(T):
            return not isinstance(T, int) or T > 0

        easy = [w for w, n in slots.items() if n >= 8 and len(w) == 2 and w[0][1] > 0]
        by_pool = [easy[-n:] for n in POOL_SLOTS]
        DVE_SLOTS = [NSLOT - 8 - n for n in POOL_SLOTS]

        g_blocks = []
        for (h, v), f in F_SIGN.items():
            for r in range(4):
                r1, r0 = divmod(r, 2)
                terms = [(4 * (h ^ v) + 2 * a + (r0 ^ (f[2 * a] != f[2 * a + 1])), f[2 * a] * (1, parity(r1))[a])
                         for a in range(2)]
                g_blocks.append((down_u[:, :, v, r, h, :], tuple(terms)))
        g_of_dve = [b for b in g_blocks if b[1][0][1] < 0 and b[1][1][1] < 0]
        g_of_pool = [b for b in g_blocks if b not in g_of_dve]

        def back_to_outputs(eng, T, s, r0, halves=range(2)):
            n = SUB * T + s
            if r0 == 0:
                eng.wait_ge(c_added, n + SUB + 1)
                eng.wait_ge(wd_ready, n + SUB + 1)
            o = rows_of(T)[:, s, :].rearrange("p (h a b o) -> p h a b o", h=2, a=2, b=2)
            for h in halves:
                for k0 in range(2):
                    signs = [RHO[4 * h + 2 * k1 + k0] * parity(k0 & r0) for k1 in range(2)]
                    k1_runs = [(slice(0, 2), signs[0])] if signs[0] == signs[1] else [
                        (slice(k1, k1 + 1), signs[k1]) for k1 in range(2)]
                    for k1, sign in k1_runs:
                        dst = o[:, h, k1, k0, :]
                        last = eng.tensor_tensor(dst, dst, wd_of(T, s)[:, k1, r0, h, :],
                                                 ALU.add if sign > 0 else ALU.subtract)
            return last

        block = ctx.enter_context(nc.Block())

        @block.sync
        def _(sp):
            def load_x(T):
                if later(T):
                    sp.wait_ge(y_done, 4 * T)
                sp.dma_start(x_in[:], xr[bass.ds(T * TOK, TOK), :].rearrange("(s p) t -> p s t", p=P)
                             ).then_inc(x_loaded, 16)

            def load_cond(T):
                for b in range(BPT):
                    h = b % 2
                    which = sp.value_load(idx_sb[0:1, bass.ds(T * BPT + b, 1)], min_val=0,
                                          max_val=cond_w.shape[0] - 1)
                    sp.dma_start(cond_bd[C * h:C * h + C, b // 2, C * h:C * h + C],
                                 cond_w[bass.ds(which, 1), :, :].rearrange("a c d -> (a c) d")
                                 ).then_inc(cond_loaded, 16)

            def load_residual(T):
                if isinstance(T, int) and T == NT - 1:
                    sp.wait_ge(h_lo_ready, NC * T + 4)
                    sp.wait_ge(z_lo_ready, NR * T + 3)
                elif later(T):
                    sp.wait_ge(out_stored, 16 * SUB * T)
                sp.dma_start(rows_of(T), xr[bass.ds(T * TOK, TOK), :].rearrange("(s p) t -> p s t", p=P)
                             ).then_inc(residual_loaded, 16)

            def store(T, s):
                sp.wait_ge(o_ready, SUB * T + s + 2)
                sp.dma_start(outr[bass.ds(T * TOK + s * P, P), :], rows_of(T)[:, s, :]).then_inc(out_stored, 16)

            sp.dma_start(idx_sb[:], cond.rearrange("(a b) -> a b", a=1)).then_inc(idx_loaded, 16)
            for w in range(NQ):
                sp.dma_start(raw[0][:, w], w_gate[:, WIN[w]:WIN[w] + P, :].rearrange("j o d -> o j d")
                             ).then_inc(gate_loaded[w], 16)
            load_x(0)
            sp.wait_ge(idx_loaded, 16)
            sp.wait_ge(cond_zeroed, 1)
            load_cond(0)
            for w in range(NQ):
                sp.dma_start(raw[1][:, w], w_up[:, WIN[w]:WIN[w] + P, :].rearrange("j o d -> o j d")
                             ).then_inc(up_loaded[w], 16)
            sp.dma_start(raw_down, w_down.rearrange("j o d -> o j d")).then_inc(down_loaded, 16)
            load_x(1)
            load_cond(1)
            sp.wait_ge(transposed, 3 * NQ)
            load_residual(0)
            load_x(2)
            load_cond(2)
            store(0, 0)
            with sp.Fori(2, NT - 1) as T:
                load_x(T + 1)
                load_cond(T + 1)
                store(T - 2, 1)
                load_residual(T - 1)
                store(T - 1, 0)
            store(NT - 3, 1)
            load_residual(NT - 2)
            load_residual(NT - 1)
            store(NT - 2, 0)
            store(NT - 2, 1)
            store(NT - 1, 0)
            for h in range(2):
                sp.wait_ge(o_ready, SUB * NT + h + 1)
                sp.dma_start(outr[bass.ds((NT - 1) * TOK + P, P), h * HALF:(h + 1) * HALF],
                             rows_of(NT - 1)[:, 1, h * HALF:(h + 1) * HALF]).then_inc(out_stored, 16)
            sp.wait_ge(out_stored, 16 * (SUB * NT + 1))

        @block.gpsimd
        def _(pool):
            pool.memset(ones[:], 1.0).then_inc(ones_set, 1)
            pool.memset(ones_w2[:], 1.0).then_inc(ones_set, 1)
            pool.memset(ident[:], 0.0).then_inc(ones_set, 1)
            pool.memset(cond_bd[:], 0.0).then_inc(cond_zeroed, 1)
            pool.wait_ge(ones_set, 3)
            pool.memset(ones_w2[0:DUP, :], 0.0).then_inc(ones_set, 1)
            pool.affine_select(out=ident[:], in_=ident[:], compare_op=ALU.not_equal, fill=1.0, base=0,
                               pattern=[[-1, P]], channel_multiplier=1).then_inc(ident_set, 1)

            def signed_add(dst, a, b, sign):
                return pool.tensor_tensor(dst, a, b, ALU.add if sign > 0 else ALU.subtract)

            def all_max(T, own_ready, own, everyone, done):
                pool.wait_ge(own_ready, T + 1)
                pool.sem_inc(reduce_due, 1)
                pool.partition_all_reduce(everyone, own, P, bass.bass_isa.ReduceOp.max).then_inc(done, 1)

            def all_max_h(T):
                all_max(T, h_max1_ready, h_max1, h_all, h_all_ready)

            def all_max_y(T):
                all_max(T, y_max_ready, y_max, y_all, y_all_ready)

            def sum_y(T):
                pool.wait_ge(y_copied, 4 * T + 4)
                if later(T):
                    pool.wait_ge(y_ready, 3 * T)
                for lo, hi in ((0, 1), (1, 2), (2, 4)):
                    signed_add(y_f[:, 8 + lo:8 + hi], y_f[:, lo:hi], y_f[:, 4 + lo:4 + hi], TAU[lo]
                               ).then_inc(y_summed, 1)
                pool.wait_ge(y_summed, 5 * T + 3)
                for b in range(2):
                    signed_add(y_f[:, 12 + b], y_f[:, 8 + 2 * b], y_f[:, 9 + 2 * b], T2[b]
                               ).then_inc(y_summed, 1)
            assert TAU[2] == TAU[3]

            def pairs(T, k):
                pool.wait_ge(h_ready, NC * T + 4 * (k // 2) + 4)
                pool.wait_ge(z_ready, NR * T + k + 1)
                pair_up(pool, signed_add, h_pairs, k).then_inc(pairs_ready, 1)

            def finish(T, k):
                pool.wait_ge(pairs_ready, NR * T + k + 1)
                pool.wait_ge(z_lo_ready, NR * T + k + 1)
                finish_round(signed_add, round_buffer(T, k), h_pairs).then_inc(z_ready, 1)

            def round_of_last_tile(k):
                T, i = NT - 1, LAST_OF_POOL.index(k)
                if k == 0:
                    pool.wait_ge(y_done, 4 * NT)
                    pool.wait_ge(y_ready, 3 * NT)
                    pool.wait_ge(z_lo_ready, NR * T + 1)
                pool.wait_ge(z_ready, NR * T + i + 1)
                pair_up(pool, signed_add, h_pairs, k).then_inc(pairs_ready, 1)
                pool.wait_ge(pairs_ready, NR * T + i + 1)
                finish_round(signed_add, round_buffer(T, k), h_pairs).then_inc(z_ready, 1)

            def back(T, s):
                back_to_outputs(pool, T, s, 0).then_inc(w_added, 1)
                pool.wait_ge(w_added, SUB * T + s + 1)
                back_to_outputs(pool, T, s, 1).then_inc(o_ready, 1)

            def first_rounds(T):
                pairs(T, 0)
                finish(T, 0)
                pairs(T, 1)

            def other_rounds(T):
                for k in range(1, NR):
                    finish(T, k)
                    if k + 1 < NR:
                        pairs(T, k + 1)

            def add_terms(dst, get, w):
                (ja, sa), (jb, sb_) = w
                return signed_add(dst, get(ja), get(jb), sb_) if sa > 0 else signed_add(dst, get(jb), get(ja), -1)

            def build_slots(m):
                t = table[m]
                pool.wait_ge(turned, NQ * (m + 1))
                for w in by_pool[m]:
                    add_terms(t[:, slots[w]], lambda j: t[:, j], w).then_inc(slots_by_pool, 1)

            def down_weights():
                pool.wait_ge(turned, 3 * NQ)
                pool.memset(down_t[0:DUP, NQ - 1], 0.0).then_inc(dup_zeroed, 1)
                pool.wait_ge(dup_zeroed, 1)
                for r0 in range(2):
                    signed_add(down_pairs[:, :, r0::2, :], down_t[:, :, 0::2, :], down_t[:, :, 1::2, :],
                               parity(r0)).then_inc(down_paired, 1)
                pool.wait_ge(down_paired, 2)
                for dst, w in g_of_pool:
                    add_terms(dst, lambda j: down_pairs[:, :, j, :], w).then_inc(down_g_ready, 1)

            pool.sem_inc(z_ready, 1)
            all_max_y(0)
            sum_y(0)
            build_slots(0)
            build_slots(1)
            down_weights()
            sum_y(1)
            all_max_y(1)
            all_max_h(0)
            first_rounds(0)
            with pool.Fori(1, NT - 1) as T:
                other_rounds(T - 1)
                sum_y(T + 1)
                all_max_y(T + 1)
                all_max_h(T)
                first_rounds(T)
            other_rounds(NT - 2)
            all_max_h(NT - 1)
            for k in LAST_OF_POOL:
                round_of_last_tile(k)
            back(NT - 2, 0)

        @block.scalar
        def _(act):
            def copy_y(T, r):
                act.wait_ge(y_done, 4 * T + r + 1)
                if later(T):
                    act.wait_ge(y_ready, 3 * T)
                act.activation(y_f[:, 2 * r:2 * r + 2, :], bank_y(T, r), ACT.Copy).then_inc(y_copied, 1)

            def y_hi(T, pieces=range(len(Y_PIECES))):
                act.wait_ge(y_chain, 4 * T + 4)
                act.wait_ge(y_summed, 5 * T + 5)
                if later(T):
                    act.wait_ge(products, 3 * NC * T - 2)
                for i in pieces:
                    ops = Y_PIECES[i]
                    if later(T) and i == 1:
                        act.wait_ge(products, 3 * NC * T)
                    act.activation(y_op[:, ops, 0, :], y_f[:, ops], ACT.Copy, scale=y_up
                                   ).then_inc(y_hi_ready, 1)

            def h_hi(T, c):
                if c == 0:
                    act.wait_ge(h_chain, 4 * (T + 1))
                    if not (isinstance(T, int) and T == NT - 1):
                        act.wait_ge(down_done, SUB * (T + 1))
                act.activation(h_op[:, c, :, 0, :], h_f[:, c], ACT.Copy, scale=h_up).then_inc(h_hi_ready, 1)

            def z_hi(T, k):
                if not (isinstance(T, int) and T == NT - 1):
                    act.wait_ge(z_ready, NR * T + k + 2)
                elif k in LAST_OF_POOL:
                    act.wait_ge(z_ready, NR * T + LAST_OF_POOL.index(k) + 2)
                else:
                    act.wait_ge(z_ready_last, LAST_OF_DVE.index(k) + 1)
                act.activation(z_op[:, k, 0], round_buffer(T, k), ACT.Copy, scale=h_up).then_inc(z_hi_ready, 1)

            def chunk(T, c):
                n, u = NC * T + c, NU * T + c // 2
                if c % 2 == 0:
                    act.wait_ge(q_done, u + 1)
                    if later(T) or c > 0:
                        act.wait_ge(p_ready, n)
                    act.activation(q_sb[:], bank_q, ACT.Copy).then_inc(q_copied, 1)
                if later(T):
                    h_hi(T - 1, c)
                    if c % 2 == 0:
                        z_hi(T - 1, c // 2)
                if c == 0:
                    act.wait_ge(ffn_scales_set, 2 * (T + 1))
                if c == NC - 1 and not later(T):
                    y_hi(1)
                act.wait_ge(g_ready, n + 1)
                act.activation(g_sb[:, c % 2], g_sb[:, c % 2], ACT.Silu, scale=gate_scale
                               ).then_inc(silu_ready, 1)

            def copy_down(T, sub_tiles=range(SUB)):
                for s in sub_tiles:
                    if isinstance(T, int) and (T, s) == (NT - 1, SUB - 1):
                        act.wait_ge(last_u1_done, 1)
                    else:
                        act.wait_ge(down_done, SUB * (T + 1) + s + 1)
                    act.wait_ge(down_scale_ready, T + 1)
                    act.wait_ge(wd_ready, SUB * T + s + SUB)
                    act.activation(ud_sb[:], down_banks(s)["u1"], ACT.Copy, scale=down_scale
                                   ).then_inc(ud_ready, 1)

            def turned_out(n, dst, w):
                act.wait_ge(transposed, n + 1)
                act.activation(dst, bank_t(w), ACT.Copy).then_inc(turned, 1)

            def sum_abs(n, src, size, dst):
                if n > 0:
                    act.wait_ge(abs_summed, n)
                act.activation(junk[:, 0:size], src, ACT.Abs, accum_out=dst).then_inc(abs_summed, 1)

            act.sem_inc(ud_ready, SUB)
            act.wait_ge(ones_set, 1)
            act.activation(warm, ones[:, 0:1], ACT.Silu)
            for w in range(NQ):
                act.wait_ge(gate_loaded[w], 16)
                sum_abs(w, raw[0][:, w].rearrange("p j d -> p (j d)"), 8 * P, abs_sum[0][:, w:w + 1])
            def sum_abs_up(w):
                act.wait_ge(up_loaded[w], 16)
                sum_abs(NQ + w, raw[1][:, w].rearrange("p j d -> p (j d)"), 8 * P, abs_sum[1][:, w:w + 1])

            copy_y(0, 0)
            copy_y(0, 1)
            copy_y(0, 2)
            sum_abs_up(0)
            copy_y(0, 3)
            sum_abs_up(1)
            sum_abs_up(2)
            for w in range(NQ):
                turned_out(w, table[0][:, 0:8, w, :], 3 + w)
            act.wait_ge(down_loaded, 16)
            sum_abs(2 * NQ, raw_down.rearrange("p j d -> p (j d)"), 8 * H8, abs_sum[2])
            for w in range(NQ):
                turned_out(NQ + w, table[1][:, 0:8, w, :], w)
            y_hi(0)
            for c in range(NC):
                chunk(0, c)
                if c in TURN_AFTER:
                    w = TURN_AFTER[c]
                    act.wait_ge(tern_ready, 1)
                    turned_out(2 * NQ + w, down_t[:, w], Y_BANK)
                if c in Y_AFTER_FIRST:
                    for r in Y_AFTER_FIRST[c]:
                        copy_y(1, r)
                if c > max(TURN_AFTER):
                    act.wait_ge(dup_zeroed, 1)
                    n = -(-len(corr) // (NC - max(TURN_AFTER) - 2))
                    i = n * (c - max(TURN_AFTER) - 1)
                    for (h, v, p), (_, w) in list(corr.items())[i:i + n]:
                        (j, eight), = w
                        act.activation(down_c[:, :, v, p, h, :], down_t[:, :, j, :], ACT.Copy, scale=float(eight)
                                       ).then_inc(down_c_ready, 1)
            act.wait_ge(down_c_ready, len(corr))
            act.wait_ge(down_g_ready, len(g_of_pool))
            act.wait_ge(down_g_ready_dve, len(g_of_dve))
            with act.Fori(1, NT - 1) as T:
                for c in range(NC):
                    chunk(T, c)
                    if c in Y_AFTER:
                        copy_y(T + 1, Y_AFTER[c])
                y_hi(T + 1)
                copy_down(T - 1)
            for c in range(NC):
                chunk(NT - 1, c)
            copy_down(NT - 2, range(1))
            for w in range(NQ):
                if w < NQ - 1:
                    act.wait_ge(parts_read, w + 1)
                else:
                    copy_down(NT - 2, range(1, 2))
                for c in range(4 * w, 4 * w + 4):
                    h_hi(NT - 1, c)
                for k in range(2 * w, 2 * w + 2):
                    z_hi(NT - 1, k)
            copy_down(NT - 1)

        @block.vector
        def _(dve):
            counts = (8 * H8 * P,) * 3

            def signed_add(dst, a, b, sign):
                return dve.tensor_tensor(dst, a, b, ALU.add if sign > 0 else ALU.subtract)

            def scales(m):
                dve.wait_ge(total_ready, m + 1)
                for dst, f in ((scale[m], 1.0), (half[m], 0.5), (minus_half[m], -0.5)):
                    dve.tensor_scalar(dst, total, f / counts[m], None, ALU.mult).then_inc(scale_ready, 1)

            def ternary(m, dst, src, part=0):
                dve.wait_ge(scale_ready, 3 * (m + 1))
                dve.tensor_scalar(dst, src, minus_half[m], None, ALU.is_lt).then_inc(compared, 1)
                dve.wait_ge(compared, m + part + 1)
                dve.scalar_tensor_tensor(out=dst, in0=src, scalar=half[m], in1=dst, op0=ALU.is_gt,
                                         op1=ALU.subtract).then_inc(tern_ready, 1)

            def combine(dst, get, w):
                if len(w) == 1:
                    return dve.tensor_scalar(dst, get(w[0][0]), float(w[0][1]), None, ALU.mult)
                (ja, sa), (jb, sb_) = w
                if sa > 0:
                    return signed_add(dst, get(ja), get(jb), sb_)
                if sb_ > 0:
                    return signed_add(dst, get(jb), get(ja), -1)
                return dve.scalar_tensor_tensor(out=dst, in0=get(ja), scalar=-1.0, in1=get(jb), op0=ALU.mult,
                                                op1=ALU.subtract)

            def build_table(m):
                t = table[m]
                dve.wait_ge(turned, NQ * (m + 1))
                for w, s in slots.items():
                    if s >= 8 and w not in by_pool[m]:
                        combine(t[:, s], lambda j: t[:, j], w).then_inc(slots_built, 1)

            def y_scale(T):
                dve.wait_ge(y_copied, 4 * T + 4)
                dve.tensor_reduce(y_max, y_f[:, 0:8, :], AX.XY, ALU.max, apply_absolute_value=True
                                  ).then_inc(y_max_ready, 1)

            def power_of_two(T, all_ready, everyone, pow2, down, up, chain):
                dve.wait_ge(all_ready, T + 1)
                dve.tensor_scalar(everyone, everyone, 2.0 ** -100, None, ALU.max).then_inc(chain, 1)
                dve.wait_ge(chain, 4 * T + 1)
                dve.tensor_scalar(pow2.bitcast(I32), everyone.bitcast(I32), 0x7F800000, None, ALU.bitwise_and
                                  ).then_inc(chain, 1)
                dve.wait_ge(chain, 4 * T + 2)
                dve.tensor_scalar(down, pow2, 1.0 / TOP, None, ALU.mult).then_inc(chain, 1)
                dve.wait_ge(chain, 4 * T + 3)
                dve.reciprocal(up, down).then_inc(chain, 1)

            def y_power(T):
                power_of_two(T, y_all_ready, y_all, y_pow, y_down, y_up, y_chain)

            def h_power(T):
                power_of_two(T, h_all_ready, h_all, h_pow, h_down, h_up, h_chain)
                dve.wait_ge(h_chain, 4 * T + 4)

            def ffn_scales(T):
                dve.wait_ge(y_chain, 4 * T + 4)
                if later(T):
                    dve.wait_ge(h_ready, NC * T)
                dve.tensor_scalar(gate_scale, y_down, scale[0], None, ALU.mult).then_inc(ffn_scales_set, 1)
                dve.tensor_scalar(up_scale, y_down, scale[1], None, ALU.mult).then_inc(ffn_scales_set, 1)

            def y_lo(T, pieces):
                dve.wait_ge(y_chain, 4 * T + 4)
                for i in pieces:
                    ops = Y_PIECES[i]
                    dve.wait_ge(y_hi_ready, 3 * T + i + 1)
                    dve.scalar_tensor_tensor(out=y_op[:, ops, 1, :], in0=y_f[:, ops], scalar=y_up,
                                             in1=y_op[:, ops, 0, :], op0=ALU.mult, op1=ALU.subtract
                                             ).then_inc(y_ready, 1)

            def lo_part(dst, src, hi):
                return dve.scalar_tensor_tensor(out=dst, in0=src, scalar=h_up, in1=hi, op0=ALU.mult,
                                                op1=ALU.subtract)

            def h_lo(T, c):
                dve.wait_ge(h_hi_ready, NC * T + c + 1)
                lo_part(h_op[:, c, :, 1, :], h_f[:, c], h_op[:, c, :, 0, :]).then_inc(h_lo_ready, 1)

            def z_lo(T, k):
                dve.wait_ge(z_hi_ready, NR * T + k + 1)
                lo_part(z_op[:, k, 1], round_buffer(T, k), z_op[:, k, 0]).then_inc(z_lo_ready, 1)

            def split_h(w):
                for c in range(4 * w, 4 * w + 4):
                    h_lo(NT - 1, c)

            def split_z(w):
                for k in range(2 * w, 2 * w + 2):
                    z_lo(NT - 1, k)

            def split_window(w):
                split_h(w)
                split_z(w)

            def round_of_last_tile(k):
                i = LAST_OF_DVE.index(k)
                if i == 0:
                    dve.wait_ge(h_ready, NC * NT)
                    dve.wait_ge(y_done, 4 * NT)
                    dve.wait_ge(y_ready, 3 * NT)
                else:
                    dve.wait_ge(z_ready_last, i)
                pair_up(dve, signed_add, g_sb, k).then_inc(pairs_ready_last, 1)
                dve.wait_ge(pairs_ready_last, i + 1)
                finish_round(signed_add, round_buffer(NT - 1, k), g_sb).then_inc(z_ready_last, 1)

            def add_p(dst, bank, m, K):
                pm = p_sb[:, m:m + 1, :]
                if GAM[K] > 0:
                    return dve.tensor_tensor(dst, bank, pm.broadcast_to([P, 2, TOK]), ALU.add)
                signed_add(dst[:, 0], bank[:, 0], p_sb[:, m], 1)
                return signed_add(dst[:, 1], bank[:, 1], p_sb[:, m], -1)

            def chunk(T, c, with_max):
                n, u = NC * T + c, NU * T + c // 2
                K, s = CHUNKS[c][0], c % 2
                dve.wait_ge(q_copied, u + 1)
                dve.wait_ge(products, 3 * n + 1)
                if c > 0 or later(T):
                    dve.wait_ge(u_ready, n)
                signed_add(p_sb[:], bank_pr(s), q_sb[:], G2[K // 2] if K % 2 else 1).then_inc(p_ready, 1)
                if later(T):
                    h_lo(T - 1, c)
                dve.wait_ge(p_ready, n + 1)
                dve.wait_ge(products, 3 * n + 2)
                if c >= 2 or later(T):
                    dve.wait_ge(h_ready, n - 1)
                add_p(g_sb[:, s], bank_r(s, 0), 0, K).then_inc(g_ready, 1)
                if c == NC - 1 and not later(T):
                    y_lo(1, range(1))
                dve.wait_ge(products, 3 * n + 3)
                if c > 0 or later(T):
                    dve.wait_ge(h_ready, n)
                add_p(u_sb[:], bank_r(s, 1), 1, K).then_inc(u_ready, 1)
                if later(T):
                    if c % 2 == 0:
                        z_lo(T - 1, c // 2)
                    dve.wait_ge(h_lo_ready, n - NC + 1)
                    dve.wait_ge(pairs_ready, NR * (T - 1) + 2 * (c // 4) + 2)
                if c == NC - 1 and not later(T):
                    y_lo(1, range(1, len(Y_PIECES)))
                dve.wait_ge(silu_ready, n + 1)
                dve.wait_ge(u_ready, n + 1)
                dve.scalar_tensor_tensor(out=h_f[:, c], in0=u_sb[:], scalar=up_scale, in1=g_sb[:, s],
                                         op0=ALU.mult, op1=ALU.mult).then_inc(h_ready, 1)
                if with_max:
                    dve.wait_ge(h_ready, n + 1)
                    dve.tensor_reduce(h_max[:, c:c + 1], h_f[:, c], AX.XY, ALU.max, apply_absolute_value=True
                                      ).then_inc(h_max_ready, 1)

            def h_max_of_chunks(tiles):
                dve.wait_ge(h_max_ready, NC * tiles)
                dve.tensor_reduce(h_max1, h_max, AX.X, ALU.max).then_inc(h_max1_ready, 1)

            def h_max_of_tile(T):
                dve.wait_ge(h_ready, NC * (T + 1))
                dve.tensor_reduce(h_max1, h_f[:], AX.XYZ, ALU.max, apply_absolute_value=True
                                  ).then_inc(h_max1_ready, 1)

            def set_down_scale(T):
                if later(T):
                    dve.wait_ge(wd_ready, SUB * (T + 1))
                dve.tensor_scalar(down_scale, h_down, scale[2], 0.25, ALU.mult, ALU.mult).then_inc(down_scale_ready, 1)

            def add_down(T, s):
                n = SUB * T + s
                banks = down_banks(s)
                if s == 0:
                    dve.wait_ge(residual_loaded, 16 * (T + 1))
                    dve.wait_ge(down_scale_ready, T + 1)
                the_last = isinstance(T, int) and (T, s) == (NT - 1, SUB - 1)
                if the_last:
                    dve.wait_ge(last_c_done, 1)
                else:
                    dve.wait_ge(down_done, n + SUB + 1)
                o = rows_of(T)[:, s, :].rearrange("p (h k o) -> p h k o", h=2, k=4)
                for h in range(2):
                    last = dve.scalar_tensor_tensor(out=o[:, h], in0=banks[f"c{h}"], scalar=down_scale,
                                                    in1=o[:, h], op0=ALU.mult, op1=ALU.add)
                last.then_inc(c_added, 1)
                if the_last:
                    dve.wait_ge(down_done, n + SUB + 1)
                dve.wait_ge(ud_ready, n + SUB + 1)
                if isinstance(T, int) and (T, s) == (NT - 2, SUB - 1):
                    dve.wait_ge(z_ready_last, len(LAST_OF_DVE))
                else:
                    dve.wait_ge(o_ready, n + 1)
                for k1 in range(2):
                    last = dve.scalar_tensor_tensor(out=wd_of(T, s)[:, k1], in0=banks["u0"], scalar=down_scale,
                                                    in1=ud_sb[:], op0=ALU.mult,
                                                    op1=ALU.subtract if k1 else ALU.add)
                last.then_inc(wd_ready, 1)

            dve.sem_inc(wd_ready, SUB)
            dve.sem_inc(c_added, SUB)
            dve.sem_inc(z_lo_ready, 1)
            dve.sem_inc(o_ready, 1)
            scales(0)
            ternary(0, tern[0], raw[0])
            y_scale(0)
            scales(1)
            ternary(1, tern[1], raw[1])
            y_power(0)
            ffn_scales(0)
            scales(2)
            build_table(0)
            y_lo(0, range(0, 1))
            build_table(1)
            y_lo(0, range(1, len(Y_PIECES)))
            for c in range(NC):
                chunk(0, c, with_max=True)
                if c < NQ:
                    part = slice(P * c, min(P * c + P, H8))
                    ternary(2, tern_down[:, :, part], raw_down[:, :, part], c)
                if c == G_AFTER:
                    dve.wait_ge(down_paired, 2)
                    for dst, w in g_of_dve:
                        combine(dst, lambda j: down_pairs[:, :, j, :], w).then_inc(down_g_ready_dve, 1)
                if c == Y_MAX_AFTER - 1:
                    y_scale(1)
                if c == Y_CHAIN_AFTER - 1:
                    y_power(1)
            ffn_scales(1)
            h_max_of_chunks(1)
            h_power(0)
            set_down_scale(0)

            def back(T, s, r0):
                if r0 == 1:
                    dve.wait_ge(w_added, SUB * T + s + 1)
                back_to_outputs(dve, T, s, r0).then_inc(o_ready if r0 else w_added, 1)

            def tile(T):
                for c in range(NC):
                    chunk(T, c, with_max=False)
                    if c in BACK_AFTER and (not isinstance(T, int) or T > 1):
                        back(T - 2, SUB - 1, BACK_AFTER.index(c))
                    if c == Y_MAX_AFTER:
                        y_scale(T + 1)
                    if c == Y_CHAIN_AFTER:
                        y_power(T + 1)
                ffn_scales(T + 1)
                y_lo(T + 1, range(len(Y_PIECES)))
                h_max_of_tile(T)
                h_power(T)
                add_down(T - 1, 0)
                for r0 in range(2):
                    back(T - 1, 0, r0)
                add_down(T - 1, 1)
                set_down_scale(T)

            tile(1)
            with dve.Fori(2, NT - 1) as T:
                tile(T)
            for c in range(NC):
                chunk(NT - 1, c, with_max=True)
                if c in BACK_AFTER:
                    back(NT - 3, SUB - 1, BACK_AFTER.index(c))
            h_max_of_chunks(2)
            round_of_last_tile(1)
            h_power(NT - 1)
            round_of_last_tile(3)
            add_down(NT - 2, 0)
            split_window(0)
            split_window(1)
            split_h(2)
            split_z(2)
            add_down(NT - 2, 1)
            set_down_scale(NT - 1)
            dve.wait_ge(o_ready, SUB * (NT - 2) + 2)
            for r0 in range(2):
                back(NT - 2, 1, r0)
            add_down(NT - 1, 0)
            for r0 in range(2):
                back(NT - 1, 0, r0)
            add_down(NT - 1, 1)
            for h in range(2):
                back_to_outputs(dve, NT - 1, 1, 0, range(h, h + 1)).then_inc(w_added, 1)
                dve.wait_ge(w_added, SUB * NT + h)
                back_to_outputs(dve, NT - 1, 1, 1, range(h, h + 1)).then_inc(o_ready, 1)

        @block.tensor
        def _(pe):
            def sum_abs(m):
                pe.wait_ge(abs_summed, min(3 * m + 3, 7))
                if m < 2:
                    for w in range(NQ):
                        mm = pe.matmul(total, (ones_w2 if w == NQ - 1 else ones)[:], abs_sum[m][:, w:w + 1],
                                       start=(w == 0), stop=(w == NQ - 1))
                else:
                    mm = pe.matmul(total, ones[:], abs_sum[m], start=True, stop=True)
                mm.then_inc(total_ready, 1)

            def turn(m, w, bank):
                pe.wait_ge(tern_ready, m + 1 if m < 2 else 3 + w)
                for j in range(8):
                    src = tern[m][:, w, j, :] if m < 2 else tern_down[:, j, WIN[w]:WIN[w] + P]
                    mm = pe.transpose(bank_t(bank)[:, j, :], src, ident[:])
                mm.then_inc(transposed, 1)

            def y_round(T, r):
                if r == 0:
                    pe.wait_ge(x_loaded, 16 * (T + 1))
                    pe.wait_ge(cond_loaded, 16 * BPT * (T + 1))
                if later(T):
                    pe.wait_ge(y_copied, 4 * T + r)
                for i in range(2):
                    for s in range(SUB):
                        f = P * (2 * r + i)
                        mm = pe.matmul(bank_y(T, r)[:, i, P * s:P * s + P], x_in[:, s, f:f + P], cond_bd[:, s, :],
                                       start=True, stop=True)
                mm.then_inc(y_done, 1)

            def group(dst, m, terms):
                for i, (slot, q, op) in enumerate(terms):
                    for e in range(2):
                        mm = pe.matmul(dst, table[m][:, slot, q, :], y_op[:, op, e, :],
                                       start=(i == 0 and e == 0), stop=(i == len(terms) - 1 and e == 1))
                return mm

            def gate_up(T, c):
                K, q = CHUNKS[c]
                s, n, u = c % 2, NC * T + c, NU * T + c // 2
                if c == 0:
                    pe.wait_ge(y_ready, 3 * T + 1)
                if c % 2 == 0:
                    if later(T) or c > 0:
                        pe.wait_ge(q_copied, u)
                    if c == 0 and later(T):
                        pe.wait_ge(ud_ready, SUB * (T - 1) + 1)
                    for m in range(2):
                        if m == 1 and c == 0 and not later(T):
                            pe.wait_ge(slots_built, sum(DVE_SLOTS))
                            pe.wait_ge(slots_by_pool, sum(POOL_SLOTS))
                        mm = group(bank_q[:, m], m, [(slots[wq[K // 2, b]], q, 12 + b) for b in range(2)])
                    mm.then_inc(q_done, 1)
                if c >= 2 or later(T):
                    pe.wait_ge(p_ready, n - 1)
                if c < 2 and later(T):
                    pe.wait_ge(wd_ready, SUB * (T - 1) + c + 1)
                for m in range(2):
                    mm = group(bank_pr(s)[:, m], m, [(slots[wpr[K, b][0]], q, 8 + wpr[K, b][1]) for b in range(2)])
                mm.then_inc(products, 1)
                if c == 0:
                    pe.wait_ge(y_ready, 3 * T + 3)
                if c < 2 and later(T):
                    pe.wait_ge(c_added, SUB * (T - 1) + c + 1)
                for m in range(2):
                    if c >= 2 or later(T):
                        pe.wait_ge(u_ready if m else g_ready, n - 1)
                    for h in range(2):
                        mm = group(bank_r(s, m)[:, h], m, [(slots[wr[h, K, p][0]], q, wr[h, K, p][1])
                                                           for p in range(4)])
                    mm.then_inc(products, 1)

            def down_products():
                for w in range(NQ):
                    for p in range(4):
                        for v in range(2):
                            for e in range(2):
                                for h in range(2):
                                    yield (2 * w + p // 2, False, f"c{h}", corr[h, v, p][0],
                                           h_op[:, 4 * w + p, v, e], down_c[:, w, v, p, h])
                    for v in range(2):
                        for e in range(2):
                            for r in range(4):
                                yield (2 * w + v, True, f"u{r // 2}", r % 2, z_op[:, 2 * w + v, e, r],
                                       down_u[:, w, v, r])

            products_of_down = list(down_products())
            by_bank = sorted(products_of_down, key=lambda x: ["c0", "c1", "u1", "u0"].index(x[2]))
            window_ends = [i for i, x in enumerate(products_of_down) if i + 1 == len(products_of_down)
                           or products_of_down[i + 1][0] // 2 > x[0] // 2]

            def down(T):
                done = NC * (T + 2) if not isinstance(T, int) else NC * min(T + 2, NT)
                T_int = T if isinstance(T, int) else None
                for s in range(SUB):
                    ordered = by_bank if (T_int, s) == (NT - 1, SUB - 1) else products_of_down
                    first = {bank: next(i for i, x in enumerate(ordered) if x[2] == bank)
                             for bank in ("c0", "c1", "u0", "u1")}
                    last = {x[2]: i for i, x in enumerate(ordered)}
                    banks = down_banks(s)
                    pe.wait_ge(u_ready, done - 1 + s)
                    if isinstance(T, int) and T == NT - 1:
                        if ordered is products_of_down:
                            pe.wait_ge(wd_ready, SUB * T + s + 1)
                        pe.wait_ge(ud_ready, SUB * T + s + 1)
                        pe.wait_ge(c_added, SUB * T + s + 1)
                    got = None
                    for i, (k, is_z, bank, place, operand, w) in enumerate(ordered):
                        if s == 0 and (k, is_z) != got:
                            got = (k, is_z)
                            if is_z:
                                pe.wait_ge(z_lo_ready, NR * T + k + 2)
                            else:
                                pe.wait_ge(h_lo_ready, NC * T + 2 * k + 2)
                        if ordered is by_bank and i == last["c1"] + 1:
                            pe.wait_ge(wd_ready, SUB * T + s + 1)
                        mm = pe.matmul(banks[bank][:, place], operand[:, P * s:P * s + P], w,
                                       start=(i == first[bank]), stop=(i == last[bank]), skip_group_check=True)
                        if T_int == NT - 2 and s == SUB - 1 and i in window_ends[:-1]:
                            mm.then_inc(parts_read, 1)
                        if ordered is by_bank and i == last["c1"]:
                            mm.then_inc(last_c_done, 1)
                        if ordered is by_bank and i == last["u1"]:
                            mm.then_inc(last_u1_done, 1)
                    mm.then_inc(down_done, 1)

            pe.sem_inc(down_done, SUB)
            pe.wait_ge(ones_set, 4)
            pe.wait_ge(ident_set, 1)
            sum_abs(0)
            for r in range(4):
                y_round(0, r)
            for w in range(NQ):
                turn(0, w, 3 + w)
            pe.wait_ge(scale_ready, 3)
            sum_abs(1)
            pe.wait_ge(scale_ready, 6)
            sum_abs(2)
            pe.wait_ge(y_copied, 4)
            for w in range(NQ):
                turn(1, w, w)
            pe.wait_ge(turned, 2 * NQ)
            pe.wait_ge(slots_built, DVE_SLOTS[0])
            pe.wait_ge(slots_by_pool, POOL_SLOTS[0])
            pe.wait_ge(scale_ready, 9)
            for c in range(NC):
                gate_up(0, c)
                if c in TURN_AFTER:
                    w = TURN_AFTER[c]
                    pe.wait_ge(y_copied, 4)
                    pe.wait_ge(turned, 2 * NQ + w)
                    turn(2, w, Y_BANK)
                if c in Y_AFTER_FIRST:
                    pe.wait_ge(turned, 3 * NQ)
                    for r in Y_AFTER_FIRST[c]:
                        y_round(1, r)
            pe.wait_ge(down_c_ready, len(corr))
            pe.wait_ge(down_g_ready, len(g_of_pool))
            pe.wait_ge(down_g_ready_dve, len(g_of_dve))
            with pe.Fori(1, NT - 1) as T:
                for c in range(NC):
                    gate_up(T, c)
                    if c in Y_AFTER:
                        if Y_AFTER[c] == 0:
                            pe.wait_ge(ud_ready, SUB * T)
                        y_round(T + 1, Y_AFTER[c])
                pe.wait_ge(y_copied, 4 * (T + 2))
                down(T - 1)
            for c in range(NC):
                gate_up(NT - 1, c)
            down(NT - 2)
            down(NT - 1)


_INS = ["x", "itok_B_0_15", "L0_cond_weights", "L0_ffn_w_gate", "L0_ffn_w_up", "L0_ffn_w_down"]


def kernel(**inputs):
    import numpy as _np
    import concourse.bacc as _bacc
    from concourse import mybir as _mybir
    from concourse.bass_utils import run_bass_kernel_spmd as _run

    nc = _bacc.Bacc("TRN2", target_bir_lowering=False, num_devices=1)
    arrays, args = {}, []
    for name in _INS:
        a = _np.ascontiguousarray(inputs[name])
        arrays[f"in_{name}_dram"] = a
        args.append(nc.dram_tensor(f"in_{name}_dram", a.shape, _mybir.dt.from_np(a.dtype), kind="ExternalInput").ap())
    args.append(nc.dram_tensor("out_dram", inputs["x"].shape, F32, kind="ExternalOutput").ap())
    build(nc, *args)
    r = _run(nc, [arrays], core_ids=[0])
    return r.results[0]["out_dram"]
```
